# Optimizing a Trainium2 kernel written in Bass

```python
import numpy as np
import jax
import jax.numpy as jnp

def _softmax(x, axis=-1):
    return jax.nn.softmax(x, axis=axis)

def _gelu(x):
    return jax.nn.gelu(x, approximate=True)

def _silu(x):
    return jax.nn.silu(x)

def _sigmoid(x):
    return jax.nn.sigmoid(x)

def _layernorm(x, axis=-1, eps=1e-05):
    m = jnp.mean(x, axis=axis, keepdims=True)
    v = jnp.var(x, axis=axis, keepdims=True)
    return (x - m) / jnp.sqrt(v + eps)

def _scatter_add(tgt, idx, src, axis=0):
    return tgt.at[idx].add(src)

def _segment_sum(src, seg, n):
    return jax.ops.segment_sum(src, seg, n)
kernel_name = 'mk_macaron_d2_jaxref_r8_7d0402'

def setup_inputs(seed: int=0):
    np.random.seed(seed)
    _w = jnp.asarray

    def _L0_attn_setup():
        import jax, jax.numpy as jnp
        import numpy as np
        DIM = 128
        QK = 128
        HID = 256
        B, N = (4, 256)
        EPS = 1e-05
        key = jax.random.key(seed)
        ks = jax.random.split(key, 8)
        std = 0.02
        return {'x': jax.random.normal(ks[0], (B, N, DIM), jnp.float32), 'ln_scale': jnp.ones((DIM,), jnp.float32), 'ln_bias': jnp.zeros((DIM,), jnp.float32), 'W_hidden': jax.random.normal(ks[1], (DIM, 2 * HID), jnp.float32) * std, 'b_hidden': jnp.zeros((2 * HID,), jnp.float32), 'W_qk': jax.random.normal(ks[2], (DIM, QK), jnp.float32) * std, 'b_qk': jnp.zeros((QK,), jnp.float32), 'os_weight': jax.random.normal(ks[3], (2, QK), jnp.float32) * std, 'os_bias': jnp.zeros((2, QK), jnp.float32), 'W_out': jax.random.normal(ks[4], (HID, DIM), jnp.float32) * std, 'b_out': jnp.zeros((DIM,), jnp.float32)}
    _L0_attn_in = _L0_attn_setup()

    def _L0_ffn_setup():
        import jax, jax.numpy as jnp
        import numpy as np
        DIM = 128
        HIDDEN = 256
        N_EXPERTS = 8
        TOP_K = 2
        EPS = 1e-06

        def rms_norm(x, scale, eps=EPS):
            ms = jnp.mean(jnp.square(x.astype(jnp.float32)), axis=-1, keepdims=True)
            s = scale.astype(jnp.float32) * jax.lax.rsqrt(ms + eps)
            return x * s.astype(x.dtype)

        def moe_linear(xf, ids, W):
            E = W.shape[0]
            out = jnp.zeros((xf.shape[0], W.shape[1]), dtype=xf.dtype)
            for e in range(E):
                out = out + jnp.where((ids == e)[:, None], xf @ W[e].T, 0.0)
            return out
        key = jax.random.key(seed)
        k1, k2, k3, k4 = jax.random.split(key, 4)
        x = jax.random.normal(k1, (4, 512, DIM), dtype=jnp.float32)
        norm_scale = jnp.ones((DIM,), dtype=jnp.float32)
        w_router = jax.random.normal(k2, (N_EXPERTS, DIM), dtype=jnp.float32) / np.sqrt(DIM)
        lim_up = np.sqrt(6.0 / (DIM + 2 * HIDDEN))
        w_up = jax.random.uniform(k3, (N_EXPERTS, 2 * HIDDEN, DIM), dtype=jnp.float32, minval=-lim_up, maxval=lim_up)
        lim_dn = np.sqrt(6.0 / (HIDDEN + DIM))
        w_down = jax.random.uniform(k4, (N_EXPERTS, DIM, HIDDEN), dtype=jnp.float32, minval=-lim_dn, maxval=lim_dn)
        return {'x': x, 'norm_scale': norm_scale, 'w_router': w_router, 'w_up': w_up, 'w_down': w_down}
    _L0_ffn_in = _L0_ffn_setup()

    def _L1_attn_setup():
        import jax, jax.numpy as jnp
        import numpy as np
        B, N, D, DHAT, H = (2, 256, 128, 64, 16)
        F = DHAT // H
        G = D // H

        def _phi(x):
            return jax.nn.elu(x) + 1.0

        def _linear_attention(Q, K, V):
            kv = jnp.cumsum(jnp.einsum('bhtf,bhtg->bhtfg', K, V), axis=2)
            Z = 1.0 / (jnp.einsum('bhtf,bhtf->bht', Q, jnp.cumsum(K, axis=2)) + 1e-06)
            out = jnp.einsum('bhtf,bhtfg->bhtg', Q, kv) * Z[..., None]
            return out
        key = jax.random.key(seed)
        ks = jax.random.split(key, 9)

        def lin_w(k, din, dout):
            return jax.random.normal(k, (din, dout), jnp.float32) / np.sqrt(din).astype(np.float32)
        return {'x': jax.random.normal(ks[0], (B, N, D), jnp.float32), 'wq': lin_w(ks[1], D, DHAT), 'bq': jnp.zeros((DHAT,), jnp.float32), 'wk': lin_w(ks[2], D, DHAT), 'bk': jnp.zeros((DHAT,), jnp.float32), 'wv': lin_w(ks[3], D, D), 'bv': jnp.zeros((D,), jnp.float32), 'wo': lin_w(ks[4], D, D), 'bo': jnp.zeros((D,), jnp.float32)}
    _L1_attn_in = _L1_attn_setup()

    def _L1_ffn_setup():
        import jax, jax.numpy as jnp
        import numpy as np
        EPS = 1e-06
        TOP_K = 2

        def rms_norm(x, scale, eps=EPS):
            xf = x.astype(jnp.float32)
            mean_sq = jnp.mean(xf * xf, axis=-1, keepdims=True)
            return (xf * (scale.astype(jnp.float32) * jax.lax.rsqrt(mean_sq + eps))).astype(x.dtype)
        key = jax.random.key(seed)
        k0, k1, k2, k3 = jax.random.split(key, 4)
        B, S, D, H, E = (2, 256, 128, 352, 8)
        x = jax.random.normal(k0, (B, S, D), dtype=jnp.float32)
        norm_scale = jnp.ones((D,), dtype=jnp.float32)
        w_router = jax.random.normal(k1, (E, D), dtype=jnp.float32) * 0.02
        w_up = jax.random.normal(k2, (E, 2 * H, D), dtype=jnp.float32) * 0.02
        w_down = jax.random.normal(k3, (E, D, H), dtype=jnp.float32) * 0.02
        return {'x': x, 'norm_scale': norm_scale, 'w_router': w_router, 'w_up': w_up, 'w_down': w_down}
    _L1_ffn_in = _L1_ffn_setup()
    _d = {'L0_attn_x': _L0_attn_in['x'], 'L0_attn_ln_scale': _L0_attn_in['ln_scale'], 'L0_attn_ln_bias': _L0_attn_in['ln_bias'], 'L0_attn_W_hidden': _L0_attn_in['W_hidden'], 'L0_attn_b_hidden': _L0_attn_in['b_hidden'], 'L0_attn_W_qk': _L0_attn_in['W_qk'], 'L0_attn_b_qk': _L0_attn_in['b_qk'], 'L0_attn_os_weight': _L0_attn_in['os_weight'], 'L0_attn_os_bias': _L0_attn_in['os_bias'], 'L0_attn_W_out': _L0_attn_in['W_out'], 'L0_attn_b_out': _L0_attn_in['b_out'], 'L0_ffn_norm_scale': _L0_ffn_in['norm_scale'], 'L0_ffn_w_router': _L0_ffn_in['w_router'], 'L0_ffn_w_up': _L0_ffn_in['w_up'], 'L0_ffn_w_down': _L0_ffn_in['w_down'], 'L1_attn_wq': _L1_attn_in['wq'], 'L1_attn_bq': _L1_attn_in['bq'], 'L1_attn_wk': _L1_attn_in['wk'], 'L1_attn_bk': _L1_attn_in['bk'], 'L1_attn_wv': _L1_attn_in['wv'], 'L1_attn_bv': _L1_attn_in['bv'], 'L1_attn_wo': _L1_attn_in['wo'], 'L1_attn_bo': _L1_attn_in['bo'], 'L1_ffn_norm_scale': _L1_ffn_in['norm_scale'], 'L1_ffn_w_router': _L1_ffn_in['w_router'], 'L1_ffn_w_up': _L1_ffn_in['w_up'], 'L1_ffn_w_down': _L1_ffn_in['w_down']}
    _x0 = _d['L0_attn_x']
    _d['L0_attn_x'] = jax.random.normal(jax.random.fold_in(jax.random.key(seed), 1), (8, 256, 128), dtype=_x0.dtype)
    del _x0
    return _d

def reference(L0_attn_x, L0_attn_ln_scale, L0_attn_ln_bias, L0_attn_W_hidden, L0_attn_b_hidden, L0_attn_W_qk, L0_attn_b_qk, L0_attn_os_weight, L0_attn_os_bias, L0_attn_W_out, L0_attn_b_out, L0_ffn_norm_scale, L0_ffn_w_router, L0_ffn_w_up, L0_ffn_w_down, L1_attn_wq, L1_attn_bq, L1_attn_wk, L1_attn_bk, L1_attn_wv, L1_attn_bv, L1_attn_wo, L1_attn_bo, L1_ffn_norm_scale, L1_ffn_w_router, L1_ffn_w_up, L1_ffn_w_down):

    def _L0_attn_ref(x, ln_scale, ln_bias, W_hidden, b_hidden, W_qk, b_qk, os_weight, os_bias, W_out, b_out):
        import jax, jax.numpy as jnp
        import numpy as np
        DIM = 128
        QK = 128
        HID = 256
        B, N = (4, 256)
        EPS = 1e-05
        n = x.shape[1]
        mu = jnp.mean(x, axis=-1, keepdims=True)
        var = jnp.mean(jnp.square(x - mu), axis=-1, keepdims=True)
        xn = (x - mu) / jnp.sqrt(var + EPS) * ln_scale + ln_bias
        hid = jax.nn.silu(xn @ W_hidden + b_hidden)
        v, gate = (hid[..., :HID], hid[..., HID:])
        qk = jax.nn.silu(xn @ W_qk + b_qk)
        qk2 = qk[..., None, :] * os_weight + os_bias
        q, k = (qk2[..., 0, :], qk2[..., 1, :])
        sim = jnp.einsum('bid,bjd->bij', q, k) / n
        attn = jnp.square(jax.nn.relu(sim))
        out = jnp.einsum('bij,bjd->bid', attn, v)
        out = out * gate
        return out @ W_out + b_out

    def _L0_ffn_ref(x, norm_scale, w_router, w_up, w_down):
        import jax, jax.numpy as jnp
        import numpy as np
        DIM = 128
        HIDDEN = 256
        N_EXPERTS = 8
        TOP_K = 2
        EPS = 1e-06

        def rms_norm(x, scale, eps=EPS):
            ms = jnp.mean(jnp.square(x.astype(jnp.float32)), axis=-1, keepdims=True)
            s = scale.astype(jnp.float32) * jax.lax.rsqrt(ms + eps)
            return x * s.astype(x.dtype)

        def moe_linear(xf, ids, W):
            E = W.shape[0]
            out = jnp.zeros((xf.shape[0], W.shape[1]), dtype=xf.dtype)
            for e in range(E):
                out = out + jnp.where((ids == e)[:, None], xf @ W[e].T, 0.0)
            return out
        B, S, D = x.shape
        skip = x
        xn = rms_norm(x, norm_scale)
        scores = (xn @ w_router.T).astype(jnp.float32)
        scores_topk, idx = jax.lax.top_k(scores, TOP_K)
        weights = jax.nn.softmax(scores_topk, axis=-1)
        xf = jnp.broadcast_to(xn[..., None, :], (B, S, TOP_K, D)).reshape(-1, D)
        ids = idx.reshape(-1)
        up = moe_linear(xf, ids, w_up)
        u, gate = jnp.split(up, 2, axis=-1)
        h = u * jax.nn.silu(gate)
        down = moe_linear(h, ids, w_down)
        down = down.reshape(B, S, TOP_K, D)
        out = jnp.sum(down * weights[..., None].astype(down.dtype), axis=-2)
        return out + skip

    def _L1_attn_ref(x, wq, bq, wk, bk, wv, bv, wo, bo):
        import jax, jax.numpy as jnp
        import numpy as np
        B, N, D, DHAT, H = (2, 256, 128, 64, 16)
        F = DHAT // H
        G = D // H

        def _phi(x):
            return jax.nn.elu(x) + 1.0

        def _linear_attention(Q, K, V):
            kv = jnp.cumsum(jnp.einsum('bhtf,bhtg->bhtfg', K, V), axis=2)
            Z = 1.0 / (jnp.einsum('bhtf,bhtf->bht', Q, jnp.cumsum(K, axis=2)) + 1e-06)
            out = jnp.einsum('bhtf,bhtfg->bhtg', Q, kv) * Z[..., None]
            return out
        Bx, Nx, Dx = x.shape
        Q = (x @ wq + bq).reshape(Bx, Nx, H, F).transpose(0, 2, 1, 3)
        K = (x @ wk + bk).reshape(Bx, Nx, H, F).transpose(0, 2, 1, 3)
        V = (x @ wv + bv).reshape(Bx, Nx, H, G).transpose(0, 2, 1, 3)
        Q, K = (_phi(Q), _phi(K))
        out = _linear_attention(Q, K, V)
        out = out.transpose(0, 2, 1, 3).reshape(Bx, Nx, Dx)
        return out @ wo + bo

    def _L1_ffn_ref(x, norm_scale, w_router, w_up, w_down):
        import jax, jax.numpy as jnp
        import numpy as np
        EPS = 1e-06
        TOP_K = 2

        def rms_norm(x, scale, eps=EPS):
            xf = x.astype(jnp.float32)
            mean_sq = jnp.mean(xf * xf, axis=-1, keepdims=True)
            return (xf * (scale.astype(jnp.float32) * jax.lax.rsqrt(mean_sq + eps))).astype(x.dtype)
        skip = x
        xn = rms_norm(x, norm_scale)
        scores = jnp.einsum('bsd,ed->bse', xn, w_router)
        _, ids = jax.lax.top_k(scores, TOP_K)
        probs = jax.nn.softmax(scores, axis=-1)
        c = jnp.take_along_axis(probs, ids, axis=-1)
        h = jnp.einsum('bsd,ehd->bseh', xn, w_up)
        val, gate = jnp.split(h, 2, axis=-1)
        h = val * jax.nn.silu(gate)
        y = jnp.einsum('bseh,edh->bsed', h, w_down)
        yk = jnp.take_along_axis(y, ids[..., None], axis=2)
        out = jnp.sum(yk * c[..., None], axis=2)
        return out + skip
    x = L0_attn_x
    x = x + 0.5 * _L0_ffn_ref(_layernorm(x, axis=-1), L0_ffn_norm_scale, L0_ffn_w_router, L0_ffn_w_up, L0_ffn_w_down)
    x = x + _L0_attn_ref(_layernorm(x, axis=-1), L0_attn_ln_scale, L0_attn_ln_bias, L0_attn_W_hidden, L0_attn_b_hidden, L0_attn_W_qk, L0_attn_b_qk, L0_attn_os_weight, L0_attn_os_bias, L0_attn_W_out, L0_attn_b_out)
    x = x + 0.5 * _L0_ffn_ref(_layernorm(x, axis=-1), L0_ffn_norm_scale, L0_ffn_w_router, L0_ffn_w_up, L0_ffn_w_down)
    x = x + 0.5 * _L1_ffn_ref(_layernorm(x, axis=-1), L1_ffn_norm_scale, L1_ffn_w_router, L1_ffn_w_up, L1_ffn_w_down)
    x = x + _L1_attn_ref(_layernorm(x, axis=-1), L1_attn_wq, L1_attn_bq, L1_attn_wk, L1_attn_bk, L1_attn_wv, L1_attn_bv, L1_attn_wo, L1_attn_bo)
    x = x + 0.5 * _L1_ffn_ref(_layernorm(x, axis=-1), L1_ffn_norm_scale, L1_ffn_w_router, L1_ffn_w_up, L1_ffn_w_down)
    return x

_drawn_inputs = setup_inputs


def setup_inputs(seed=0):
    import zlib

    import numpy as np

    out = dict(_drawn_inputs(seed))
    spreads = {'L0_attn_ln_scale': (1.0, 0.2),
     'L0_attn_ln_bias': (0.0, 0.1),
     'L0_attn_b_hidden': (0.0, 0.1),
     'L0_attn_b_qk': (0.0, 0.1),
     'L0_attn_os_bias': (0.0, 0.1),
     'L0_attn_b_out': (0.0, 0.1),
     'L0_ffn_norm_scale': (1.0, 0.2),
     'L1_attn_bq': (0.0, 0.8),
     'L1_attn_bk': (0.0, 0.8),
     'L1_attn_bv': (0.0, 0.1),
     'L1_attn_bo': (0.0, 0.1),
     'L1_ffn_norm_scale': (1.0, 0.6)}
    factors = {'L1_attn_wq': 4.594, 'L1_ffn_w_router': 8.0, 'L1_ffn_w_up': 8.0, 'L1_ffn_w_down': 8.0}
    for name, (base, spread) in spreads.items():
        noise = np.random.default_rng([zlib.crc32(name.encode()), seed]).standard_normal(out[name].shape)
        drawn = base * np.exp(spread * noise) if base else spread * noise
        out[name] = jnp.asarray(drawn.astype(out[name].dtype))
    for name, factor in factors.items():
        out[name] = (out[name] * factor).astype(out[name].dtype)
    return out
```

```python
import concourse.bass as bass
from concourse import mybir
from contextlib import ExitStack

F32 = mybir.dt.float32
F32R = mybir.dt.float32r
ALU = mybir.AluOpType
ACT = mybir.ActivationFunctionType
AX = mybir.AxisListType

P = 128
NT = 512
TB = NT // P
E = 8
SEQ = 256
HID = 256
HEADS, F, G = 16, 4, 8
LAG = 3
RING = 4
HUGE = 3.0e38


class Experts:

    def __init__(self, hidden):
        self.hidden = hidden
        self.rows = [min(P, hidden - c * P) for c in range((hidden + P - 1) // P)]
        self.chunks = len(self.rows)
        self.steps = E * self.chunks

    def up_at(self, e, c):
        return e * 2 * self.hidden + c * 2 * P

    def down_at(self, e, c):
        return (c * E + e) * P


def after(eng, sem, count):
    if not (isinstance(count, int) and count <= 0):
        eng.wait_ge(sem, count)


def after_apart(eng, cell, sem, count, copied=None):
    eng.wait_ge(sem, count)
    if not isinstance(count, int):
        if copied is None:
            eng.memset(cell, 0.0)
        else:
            eng.tensor_tensor(cell, copied, copied, ALU.mult)


class Links:

    def __init__(self, eng, sem, base):
        self.eng, self.sem, self.base, self.n = eng, sem, base, 0

    def __call__(self, ins, apart=None):
        self.n += 1
        ins.then_inc(self.sem, 1)
        if apart is None:
            self.eng.wait_ge(self.sem, self.base + self.n)
        else:
            after_apart(self.eng, apart, self.sem, self.base + self.n)


def macaron(nc, x, up0, down0, up1, down1a, down1b, router, norm, att0_w, att0_qk, att0_out, att0_cols,
            att0_brow, att0_orow, att1_w, att1_brow, att1_out, att1_orow, out):
    experts = [Experts(256), Experts(352)]
    layer = [0, 0, 1, 1]
    NB = x.shape[0] // NT
    steps = [experts[l].steps for l in layer]
    first_step = [NB * sum(steps[:s]) for s in range(5)]
    ctx = ExitStack()
    with ctx:
        def sb(name, cols, dt=F32, rows=P):
            return ctx.enter_context(nc.sbuf_tensor(name, [rows, cols], dt))

        def sem(name):
            return ctx.enter_context(nc.semaphore(name))

        upH = [sb(f"up{l}_hi", 2 * experts[l].hidden * E, F32R) for l in range(2)]
        upL = [sb(f"up{l}_lo", 2 * experts[l].hidden * E, F32R) for l in range(2)]
        downH = [sb(f"down{l}_hi", experts[l].chunks * E * P, F32R) for l in range(2)]
        downL = [sb(f"down{l}_lo", experts[l].chunks * E * P, F32R) for l in range(2)]
        X = sb("x_res", NB * NT)
        xH = sb("xn_hi", NB * NT, F32R)
        xL = sb("xn_lo", NB * NT, F32R)
        sg = sb("silu_gate", 2 * NT)
        hid = sb("hidden", 2 * NT)
        hH = sb("hidden_hi", RING * NT, F32R)
        hL = sb("hidden_lo", RING * NT, F32R)
        wtok = sb("token_weights", 4 * NT)
        region = sb("attention", 8 * NT)
        R = [region[:, i * NT:(i + 1) * NT] for i in range(8)]
        xT = sb("attn_xT", NT)
        spare = sb("spare", 2)
        a_st = sb("a_stats", TB * 6)
        a_mv = sb("a_meanvar", TB * 2)
        a_ve = sb("a_var", TB)
        a_rs = sb("a_rstd", TB)
        a2_st = sb("a2_stats", TB * 6)
        a2_mv = sb("a2_meanvar", TB * 2)
        a2_ve = sb("a2_var", TB)
        a2_rs = sb("a2_rstd", TB)
        kden = sb("k_den", TB * 64)
        den = sb("den", TB * HEADS)
        rden = sb("rden", TB * HEADS)
        Y = sb("ln_out", NT)
        Z = Y
        zT = Y
        b_st = sb("b_stats", TB * 6)
        b_mv = sb("b_meanvar", TB * 2)
        b_ve = sb("b_var", TB)
        b_rs = sb("b_rstd", TB)
        b_ms = sb("b_sumsq", TB)
        b_me = sb("b_meansq", TB)
        b_rr = sb("b_rrms", TB)
        m1 = sb("top1", TB)
        m2 = sb("top2", TB)
        pm = sb("pick", TB)
        e1 = sb("is_max", TB * E)
        oh1 = sb("first", TB * E)
        oh2 = sb("second", TB * E)
        rest = sb("rest", TB * E)
        th = sb("tanh", TB * E)
        thn = sb("one_minus", TB * E)
        w1 = sb("w_first", TB)
        w2 = sb("w_second", TB)
        wt = sb("w_tok", TB * E)
        wtT = sb("w_tokT", NT, rows=E)
        ident = sb("ident", P)
        ones = sb("ones", P)
        tri = sb("tri", P)
        mhalf = sb("minus_half", TB)
        prio = sb("priority", TB * E)
        wr = sb("router", 2 * E)
        wn = sb("norm", 2)
        w_hid = sb("a0_hidden", 2 * HID)
        w_qk = sb("a0_qk", P)
        w_o0 = sb("a0_out", 2 * P)
        cols0 = sb("a0_cols", 9)
        brow0 = sb("a0_brow", HID, rows=1)
        orow0 = sb("a0_orow", P, rows=1)
        w_qkv = sb("a1_qkv", 2 * P)
        w_o1 = sb("a1_out", P)
        brow1 = sb("a1_brow", 2 * P, rows=1)
        orow1 = sb("a1_orow", P, rows=1)

        UG = [ctx.enter_context(nc.psum_tensor(f"up_gate{i}", [P, 2 * NT], F32)) for i in range(2)]
        ACC = ctx.enter_context(nc.psum_tensor("acc", [P, NT], F32))
        S = [ctx.enter_context(nc.psum_tensor(f"side{i}", [P, NT], F32)) for i in range(3)]
        WD = nc.dram_tensor("token_weights_dram", [NB * E, NT], F32, kind="Internal").ap()

        x_loaded = sem("x_loaded")
        small_loaded = sem("small_loaded")
        stage_loaded = [sem(f"stage_loaded{i}") for i in range(4)]
        wtok_loaded = [sem(f"wtok_loaded{i}") for i in range(4)]
        wd_stored = sem("wd_stored")
        out_stored = sem("out_stored")
        consts = sem("consts")
        const_base = sem("const_base")
        split_hi = sem("split_hi")
        split_lo = sem("split_lo")
        up_done = sem("up_done")
        silu_done = sem("silu_done")
        hid_done = sem("hid_done")
        scaled = sem("scaled")
        hi_done = sem("hi_done")
        lo_done = sem("lo_done")
        down_done = sem("down_done")
        accT = sem("acc_evacuated")
        acc_tok = sem("acc_token_major")
        x_done = sem("x_done")
        ln1_var, ln1_rstd = sem("ln1_var"), sem("ln1_rstd")
        ln2_var, ln2_rstd = sem("ln2_var"), sem("ln2_rstd")
        yn_ready, ynT_ready, xT_ready = sem("yn_ready"), sem("ynT_ready"), sem("xT_ready")
        proj_ready, proj_used = sem("proj_ready"), sem("proj_used")
        qk_ready, sim_ready, relu_ready, sq_ready = sem("qk_ready"), sem("sim_ready"), sem("relu_ready"), sem("sq_ready")
        av_ready, og_ready, ao_ready = sem("av_ready"), sem("og_ready"), sem("ao_ready")
        qkv_ready, min_ready, v_ready, exp_ready = sem("qkv_ready"), sem("min_ready"), sem("v_ready"), sem("exp_ready")
        phi_ready, kv_ready, kcum_ready, den_read = sem("phi_ready"), sem("kv_ready"), sem("kcum_ready"), sem("den_read")
        cum_ready, cum_used = sem("cum_ready"), sem("cum_used")
        att_ready, attT_ready, attT_used = sem("att_ready"), sem("attT_ready"), sem("attT_used")
        a_link = sem("a_link")
        skip_added = sem("skip_added")
        b_var, b_rstd, y_ready, ms_ready = sem("b_var"), sem("b_rstd"), sem("y_ready"), sem("ms_ready")
        b_me_ready, rr_ready = sem("b_me_ready"), sem("rr_ready")
        z_ready, zT_ready, zT_used, xh_ready = sem("z_ready"), sem("zT_ready"), sem("zT_used"), sem("xh_ready")
        score_ready, d_ready, th_ready = sem("score_ready"), sem("d_ready"), sem("th_ready")
        w_ready, wT_ready, wT_used, xl_ready = sem("w_ready"), sem("wT_ready"), sem("wT_used"), sem("xl_ready")
        b_link = sem("b_link")

        LINKS_B = [17, 20]
        LINKS_A = [7, 10]

        def pieces(l):
            found = []
            sources = [(up0, upH[0], upL[0], 0, P), (down0, downH[0], downL[0], 0, P)] if l == 0 else \
                [(up1, upH[1], upL[1], 0, P), (down1a, downH[1], downL[1], 0, P),
                 (down1b, downH[1], downL[1], 2 * E * P, experts[1].rows[-1])]
            for src, hi, lo, at, rows in sources:
                for c in range(0, src.shape[1], NT):
                    found.append((src[:, c:c + NT], hi[0:rows, at + c:at + c + NT], lo[0:rows, at + c:at + c + NT], rows))
            return found

        pieces0 = pieces(0)
        pieces1 = pieces(1)
        split_all = pieces0 + pieces1

        def splits_of_step(j):
            n0 = len(pieces0)
            share = -(-len(pieces1) // steps[0])
            todo = range(n0 + j, len(split_all), steps[0])
            assert share <= 2
            return list(todo)

        split_order = list(range(len(pieces0))) + [i for j in range(steps[0]) for i in splits_of_step(j)]

        def each_body(eng, body):
            for s in range(4):
                body(s, 0)
                body(s, 1)
                with eng.Fori(2, NB) as b:
                    body(s, b)

        def side_after(s, b):
            return (s, b - 1) if not (isinstance(b, int) and b == 0) else (s - 1, NB - 1)

        def side_before(s, b):
            return (s, b - 2) if not (isinstance(b, int) and b < 2) else (s - 1, b + NB - 2)

        def step_of(s, b):
            return first_step[s] + b * steps[s]

        def prev_layer(s, b):
            return layer[side_after(s, b)[0]] if side_after(s, b)[0] >= 0 else None

        def xs(t, b, at=0, n=NT):
            if isinstance(b, int):
                return t[:, b * NT + at:b * NT + at + n]
            return t[:, bass.ds(b * NT + at, n)]

        def tiles(ap, cols=P):
            return ap.rearrange("p (t c) -> p t c", c=cols)

        def over(ap, n):
            return ap.unsqueeze(2).to_broadcast([ap.shape[0], ap.shape[1], n])

        block = ctx.enter_context(nc.Block())

        @block.sync
        def _(sp):
            for b in range(NB):
                sp.dma_start(tiles(xs(X, b)), x[b * NT:(b + 1) * NT, :].rearrange("(t p) d -> p t d", p=P)).then_inc(x_loaded, 16)
            for dst, src in ((wn, norm), (wr, router), (w_hid, att0_w), (w_qk, att0_qk), (w_o0, att0_out),
                             (cols0, att0_cols), (brow0, att0_brow), (orow0, att0_orow), (w_qkv, att1_w),
                             (brow1, att1_brow), (w_o1, att1_out), (orow1, att1_orow)):
                sp.dma_start(dst[:, :], src).then_inc(small_loaded, 16)

            def load_piece(n):
                src, _, _, rows = split_all[split_order[n]]
                after(sp, split_lo, n - 3)
                sp.dma_start(R[n % 4][0:rows, :], src).then_inc(stage_loaded[n % 4], 16)

            loaded = [0]
            for n in range(len(pieces0)):
                load_piece(n)

            def store_out(b):
                after(sp, x_done, 3 * NB + b + 1)
                rows = out[b * NT:(b + 1) * NT, :] if isinstance(b, int) else out[bass.ds(b * NT, NT), :]
                sp.dma_start(rows.rearrange("(t p) d -> p t d", p=P), tiles(xs(X, b))).then_inc(out_stored, 16)

            def body(s, b):
                ex = experts[layer[s]]
                m = NB * s + b
                after(sp, wd_stored, 16 * (m + 1))
                for e in range(E):
                    if e >= 4:
                        after(sp, scaled, step_of(s, b) + (e - 3) * ex.chunks)
                    elif prev_layer(s, b) is not None:
                        after(sp, scaled, step_of(s, b) - (3 - e) * experts[prev_layer(s, b)].chunks)
                    row = WD[b * E + e:b * E + e + 1, :] if isinstance(b, int) else WD[bass.ds(b * E + e, 1), :]
                    sp.dma_start(wtok[:, (e % 4) * NT:(e % 4 + 1) * NT], row.to_broadcast([P, NT])).then_inc(wtok_loaded[e % 4], 16)
                    if s == 0 and isinstance(b, int) and b == 0:
                        for n in range(len(pieces0) + e * len(pieces1) // E, len(pieces0) + (e + 1) * len(pieces1) // E):
                            load_piece(n)
                if s == 3 and not (isinstance(b, int) and b == 0):
                    store_out(b - 1)

            each_body(sp, body)
            store_out(NB - 1)
            sp.wait_ge(out_stored, 16 * NB)

        @block.gpsimd
        def _(pool):
            pool.memset(ident[:, :], 0.0).then_inc(const_base, 1)
            pool.memset(tri[:, :], 1.0).then_inc(const_base, 1)
            pool.memset(ones[:, :], 1.0).then_inc(consts, 1)
            pool.memset(mhalf[:, :], -0.5).then_inc(consts, 1)
            for e in range(E):
                last = pool.memset(tiles(prio[:, :], E)[:, :, e:e + 1], float(E - e))
            last.then_inc(consts, 1)
            pool.wait_ge(const_base, 2)
            pool.affine_select(out=ident[:, :], in_=ident[:, :], compare_op=ALU.not_equal, fill=1.0, base=0,
                               pattern=[[-1, P]], channel_multiplier=1).then_inc(consts, 1)
            pool.affine_select(out=tri[:, :], in_=tri[:, :], compare_op=ALU.is_ge, fill=0.0, base=0,
                               pattern=[[1, P]], channel_multiplier=-1).then_inc(consts, 1)
            pool.wait_ge(consts, 5)

            def before(l, j, k):
                if j == 1:
                    pool.wait_ge(b_var, k)
                    pool.tensor_tensor(b_rs[:, :], b_ve[:, :], mhalf[:, :], ALU.pow).then_inc(b_rstd, 1)
                if j == 5:
                    after_apart(pool, spare[:, 1:2], ms_ready, k, mhalf[:, 0:1])
                    pool.tensor_scalar(b_me[:, :], b_ms[:, :], 1.0 / P, 1e-6, ALU.mult, ALU.add).then_inc(b_me_ready, 1)
                    pool.wait_ge(b_me_ready, k)
                    pool.tensor_tensor(b_rr[:, :], b_me[:, :], mhalf[:, :], ALU.pow).then_inc(rr_ready, 1)
                if j == 6:
                    pool.wait_ge(skip_added, k)
                    after_apart(pool, spare[:, 1:2], rr_ready, k, mhalf[:, 0:1])
                    for t in range(TB):
                        last = pool.tensor_scalar(Z[:, t * P:(t + 1) * P], Y[:, t * P:(t + 1) * P], b_rr[:, t:t + 1], 1.0,
                                                  ALU.mult, ALU.mult)
                    last.then_inc(z_ready, 1)

            def att_after(l, j, ka):
                if j == (3 if l == 0 else 4):
                    pool.wait_ge(ln1_var, ka + 4 * l)
                    pool.tensor_tensor(a_rs[:, :], a_ve[:, :], mhalf[:, :], ALU.pow).then_inc(ln1_rstd, 1)
                if l == 0:
                    if j == 5:
                        pool.wait_ge(ln2_var, ka)
                        pool.tensor_tensor(a2_rs[:, :], a2_ve[:, :], mhalf[:, :], ALU.pow).then_inc(ln2_rstd, 1)
                    if j in (11, 12):
                        q = j - 11
                        pool.wait_ge(relu_ready, 2 * ka - 1 + q)
                        pool.tensor_tensor(R[6 + q], R[6 + q], R[6 + q], ALU.mult).then_inc(sq_ready, 1)
                elif j in (12, 13, 14, 15):
                    t = j - 12
                    if t == 0:
                        pool.wait_ge(phi_ready, ka)
                        pool.wait_ge(v_ready, 2 * ka)
                    kk = R[0][:, t * P + 64:(t + 1) * P].rearrange("p (h f) -> p h f", f=F)
                    vv = R[1][:, t * P:(t + 1) * P].rearrange("p (h g) -> p h g", g=G)
                    pool.tensor_tensor(R[3 + t].rearrange("p (h f g) -> p h f g", f=F, g=G),
                                       kk.unsqueeze(3).to_broadcast([P, HEADS, F, G]),
                                       vv.unsqueeze(2).to_broadcast([P, HEADS, F, G]), ALU.mult).then_inc(kv_ready, 1)

            def sides(s, b, j):
                sa, ba = side_after(s, b)
                if sa in (0, 2):
                    att_after(sa // 2, j, ba + 1)
                sb_, bb = side_before(s, b)
                if 0 <= sb_ < 3:
                    before(layer[sb_ + 1], j, NB * (sb_ + 1) + bb + 1)

            def prologue(k):
                for j in range(16):
                    before(0, j, k)
            prologue(1)
            with pool.Fori(2, NB + 1) as k:
                prologue(k)

            def body(s, b):
                ex = experts[layer[s]]
                n = step_of(s, b)
                for j in range(steps[s]):
                    e, c = j // ex.chunks, j % ex.chunks
                    rows = ex.rows[c]
                    if c == 0:
                        pool.wait_ge(wtok_loaded[e % 4], 16 * (2 * (NB * s + b) + e // 4 + 1))
                    pool.wait_ge(hid_done, n + j + 1)
                    h = hid[0:rows, (j % 2) * NT:(j % 2 + 1) * NT]
                    pool.tensor_tensor(h, h, wtok[0:rows, (e % 4) * NT:(e % 4 + 1) * NT], ALU.mult).then_inc(scaled, 1)
                    sides(s, b, j)

            each_body(pool, body)
            for j in range(LAG, 16):
                sides(4, 0, j)

        @block.scalar
        def _(act):
            def split_hi_piece(n):
                _, hi, _, rows = split_all[split_order[n]]
                act.wait_ge(stage_loaded[n % 4], 16 * (n // 4 + 1))
                act.activation(hi, R[n % 4][0:rows, :], ACT.Copy).then_inc(split_hi, 1)

            def before(l, j, k, b):
                if j in (3, 4):
                    if j == 3:
                        act.wait_ge(y_ready, k)
                    for t in (0, 1) if j == 3 else (2, 3):
                        last = act.activation(S[2][:, t * P:(t + 1) * P], Y[:, t * P:(t + 1) * P], ACT.Square,
                                              accum_out=b_ms[:, t:t + 1])
                    if j == 4:
                        last.then_inc(ms_ready, 1)
                if j == 8:
                    act.wait_ge(zT_ready, k)
                    act.activation(zT[:, :], S[2][:, :], ACT.Copy, scale=wn[:, l:l + 1]).then_inc(zT_used, 1)
                    act.activation(xs(xH, b), S[2][:, :], ACT.Copy, scale=wn[:, l:l + 1]).then_inc(xh_ready, 1)
                if j == 12:
                    act.wait_ge(d_ready, k)
                    if l == 0:
                        act.activation(th[:, 0:TB], w1[:, :], ACT.Tanh, scale=0.5).then_inc(th_ready, 1)
                    else:
                        act.activation(th[:, :], rest[:, :], ACT.Tanh, scale=0.5).then_inc(th_ready, 1)
                if j == 15:
                    act.wait_ge(wT_ready, k)
                    after(act, wd_stored, 16 * (k - 1))
                    act.activation(wtT[:, :], S[2][0:E, :], ACT.Copy).then_inc(wT_used, 1)
                    act.wait_ge(wT_used, k)
                    rows = WD[b * E:(b + 1) * E, :] if isinstance(b, int) else WD[bass.ds(b * E, E), :]
                    act.dma_start(rows, wtT[:, :]).then_inc(wd_stored, 16)

            def after_stage(s, b, j):
                if j == 2:
                    m = NB * s + b
                    act.wait_ge(down_done, step_of(s, b) + steps[s])
                    after(act, x_done, m)
                    act.activation(R[3], ACC[:, :], ACT.Copy).then_inc(accT, 1)

            def att_after(l, j, ka):
                if j == 7:
                    act.wait_ge(ynT_ready, ka + 4 * l)
                    if l == 0:
                        act.activation(xT[:, :], S[1][:, :], ACT.Identity, scale=cols0[:, 0:1], bias=cols0[:, 1:2]).then_inc(xT_ready, 1)
                    else:
                        act.activation(xT[:, :], S[1][:, :], ACT.Copy).then_inc(xT_ready, 1)
                if l == 0:
                    for i in {8: (0, 1), 9: (2, 3), 10: (4,)}.get(j, ()):
                        act.wait_ge(proj_ready, 5 * ka - 4 + i)
                        dst, src, bias = ((R[0], S[0], cols0[:, 2:3]), (R[2], S[1], cols0[:, 3:4]), (R[3], S[0], cols0[:, 4:5]),
                                          (R[4], S[1], 0.0), (R[5], S[0], 0.0))[i]
                        act.activation(dst, src[:, :], ACT.Silu, bias=bias).then_inc(proj_used, 1)
                    if j in (11, 12):
                        q = j - 11
                        act.wait_ge(sim_ready, 2 * ka - 1 + q)
                        act.activation(R[6 + q], S[1 - q][:, :], ACT.Relu, scale=1.0 / SEQ).then_inc(relu_ready, 1)
                else:
                    if j in (10, 11):
                        q = j - 10
                        act.wait_ge(min_ready, 2 * ka - 1 + q)
                        act.activation(tiles(R[1][:, q * SEQ:(q + 1) * SEQ]), tiles(S[q][:, :], 2 * P)[:, :, P:2 * P], ACT.Copy).then_inc(v_ready, 1)
                    if j == 11:
                        act.wait_ge(min_ready, 2 * ka)
                        act.activation(R[2], R[2], ACT.Exp).then_inc(exp_ready, 1)
                    if j == 21:
                        act.wait_ge(attT_ready, ka)
                        act.activation(R[1], S[1][:, :], ACT.Copy).then_inc(attT_used, 1)

            def sides(s, b, j):
                sa, ba = side_after(s, b)
                if sa >= 0:
                    after_stage(sa, ba, j)
                if sa in (0, 2):
                    att_after(sa // 2, j, ba + 1)
                sb_, bb = side_before(s, b)
                if 0 <= sb_ < 3:
                    before(layer[sb_ + 1], j, NB * (sb_ + 1) + bb + 1, bb)

            act.wait_ge(small_loaded, 16 * 12)
            def prologue(b):
                for j in range(16):
                    before(0, j, b + 1, b)
            prologue(0)
            with act.Fori(1, NB) as b:
                prologue(b)
            for n in range(len(pieces0)):
                split_hi_piece(n)
            done = [len(pieces0)]

            def to_hi(n, j, rows):
                act.wait_ge(scaled, n + 1)
                after(act, down_done, n + 1 - RING)
                act.activation(hH[0:rows, (j % RING) * NT:(j % RING + 1) * NT], hid[0:rows, (j % 2) * NT:(j % 2 + 1) * NT],
                               ACT.Copy).then_inc(hi_done, 1)

            def body(s, b):
                ex = experts[layer[s]]
                n = step_of(s, b)
                for j in range(steps[s]):
                    rows = ex.rows[j % ex.chunks]
                    act.wait_ge(up_done, n + j + 1)
                    after(act, hid_done, n + j - 1)
                    act.activation(sg[0:rows, (j % 2) * NT:(j % 2 + 1) * NT], UG[j % 2][0:rows, NT:2 * NT], ACT.Silu).then_inc(silu_done, 1)
                    if j:
                        to_hi(n + j - 1, j - 1, ex.rows[(j - 1) % ex.chunks])
                    elif prev_layer(s, b) is not None:
                        to_hi(n - 1, steps[side_after(s, b)[0]] - 1, experts[prev_layer(s, b)].rows[-1])
                    if s == 0 and isinstance(b, int) and b == 0:
                        for _ in splits_of_step(j):
                            split_hi_piece(done[0])
                            done[0] += 1
                    sides(s, b, j)

            each_body(act, body)
            to_hi(first_step[4] - 1, steps[3] - 1, experts[1].rows[-1])
            sides(4, 0, 2)

        @block.vector
        def _(dve):
            def split_lo_piece(n):
                _, hi, lo, rows = split_all[split_order[n]]
                dve.wait_ge(split_hi, n + 1)
                dve.tensor_tensor(lo, R[n % 4][0:rows, :], hi.bitcast(F32), ALU.subtract).then_inc(split_lo, 1)

            def stats(link, src, st, mv, ve, eps, done):
                for t in range(TB):
                    last = dve.bn_stats(st[:, 6 * t:6 * t + 6], src(t))
                link(last, apart=spare[:, 0:1])
                for t in range(TB):
                    last = dve.bn_aggr(mv[:, 2 * t:2 * t + 2], st[:, 6 * t:6 * t + 6])
                link(last)
                dve.tensor_scalar(ve[:, :], mv[:, 1:2 * TB:2], eps, None, ALU.add).then_inc(done, 1)

            def normalise(dst, src, mv, rs):
                for t in range(TB):
                    last = dve.tensor_scalar(dst[:, t * P:(t + 1) * P], src(t), mv[:, 2 * t:2 * t + 1], rs[:, t:t + 1],
                                             ALU.subtract, ALU.mult)
                return last

            def before(l, j, k, b, state):
                if j == 0:
                    base = (k - 1) * LINKS_B[0] if l == 0 else 2 * NB * LINKS_B[0] + (k - 1 - 2 * NB) * LINKS_B[1]
                    state["link"] = Links(dve, b_link, base)
                    stats(state["link"], lambda t: xs(X, b, t * P, P), b_st, b_mv, b_ve, 1e-5, b_var)
                link = state["link"]
                sc = tiles(S[2][:, 0:TB * E], E)
                v = lambda t: tiles(t[:, :], E)
                if j == 2:
                    dve.wait_ge(b_rstd, k)
                    normalise(Y, lambda t: xs(X, b, t * P, P), b_mv, b_rs).then_inc(y_ready, 1)
                if j == 3:
                    dve.wait_ge(y_ready, k)
                    dve.scalar_tensor_tensor(xs(X, b), Y[:, :], 0.5, xs(X, b), ALU.mult, ALU.add).then_inc(skip_added, 1)
                if j == 10:
                    dve.wait_ge(score_ready, k)
                    dve.wait_ge(skip_added, k)
                    link(dve.tensor_reduce(m1[:, :], sc, AX.X, ALU.max))
                    link(dve.tensor_tensor(v(e1), sc, over(m1[:, :], E), ALU.is_equal))
                    link(dve.tensor_tensor(e1[:, :], e1[:, :], prio[:, :], ALU.mult))
                    link(dve.tensor_reduce(pm[:, :], v(e1), AX.X, ALU.max))
                    link(dve.tensor_tensor(v(oh1), v(e1), over(pm[:, :], E), ALU.is_equal))
                    link(dve.scalar_tensor_tensor(v(rest), v(oh1), -HUGE, sc, ALU.mult, ALU.add))
                    link(dve.tensor_reduce(m2[:, :], v(rest), AX.X, ALU.max))
                if j == 11:
                    if l == 0:
                        dve.tensor_tensor(w1[:, :], m1[:, :], m2[:, :], ALU.subtract).then_inc(d_ready, 1)
                    link(dve.tensor_tensor(v(e1), v(rest), over(m2[:, :], E), ALU.is_equal))
                    link(dve.tensor_tensor(e1[:, :], e1[:, :], prio[:, :], ALU.mult))
                    link(dve.tensor_reduce(pm[:, :], v(e1), AX.X, ALU.max))
                    link(dve.tensor_tensor(v(oh2), v(e1), over(pm[:, :], E), ALU.is_equal))
                    if l == 1:
                        dve.tensor_tensor(v(rest), sc, over(m1[:, :], E), ALU.subtract).then_inc(d_ready, 1)
                        link(dve.tensor_tensor(oh1[:, :], oh1[:, :], oh2[:, :], ALU.add))
                if j == 12:
                    dve.wait_ge(xh_ready, k)
                    dve.tensor_tensor(xs(xL, b), zT[:, :], xs(xH, b).bitcast(F32), ALU.subtract).then_inc(xl_ready, 1)
                if j == 13:
                    dve.wait_ge(th_ready, k)
                    if l == 0:
                        link(dve.tensor_scalar(w1[:, :], th[:, 0:TB], 0.25, 0.25, ALU.mult, ALU.add))
                        link(dve.tensor_scalar(w2[:, :], th[:, 0:TB], -0.25, 0.25, ALU.mult, ALU.add))
                        link(dve.tensor_tensor(v(oh1), v(oh1), over(w1[:, :], E), ALU.mult))
                        link(dve.tensor_tensor(v(oh2), v(oh2), over(w2[:, :], E), ALU.mult))
                        dve.tensor_tensor(wt[:, :], oh1[:, :], oh2[:, :], ALU.add).then_inc(w_ready, 1)
                    else:
                        link(dve.tensor_scalar(thn[:, :], th[:, :], -1.0, 1.0, ALU.mult, ALU.add))
                        link(dve.reciprocal(thn[:, :], thn[:, :]))
                        link(dve.scalar_tensor_tensor(rest[:, :], th[:, :], 1.0, thn[:, :], ALU.add, ALU.mult))
                        link(dve.tensor_reduce(w1[:, :], v(rest), AX.X, ALU.add))
                        link(dve.reciprocal(w2[:, :], w1[:, :]))
                        link(dve.scalar_tensor_tensor(rest[:, :], rest[:, :], 0.5, oh1[:, :], ALU.mult, ALU.mult))
                        dve.tensor_tensor(v(wt), v(rest), over(w2[:, :], E), ALU.mult).then_inc(w_ready, 1)
                    assert link.n == LINKS_B[l], (l, link.n)

            def after_stage(s, b, j, link):
                if j == 3:
                    m = NB * s + b
                    dve.wait_ge(acc_tok, m + 1)
                    ins = dve.tensor_tensor(xs(X, b), xs(X, b), S[0][:, :], ALU.add)
                    if s in (0, 2):
                        link(ins, apart=spare[:, 0:1])
                    else:
                        ins.then_inc(x_done, 1)

            def att_after(l, s, b, j, ka, link):
                if j == 3:
                    stats(link, lambda t: xs(X, b, t * P, P), a_st, a_mv, a_ve, 1e-5, ln1_var)
                if j == 4 + l:
                    dve.wait_ge(ln1_rstd, ka + 4 * l)
                    last = normalise(R[0], lambda t: xs(X, b, t * P, P), a_mv, a_rs)
                    if l == 0:
                        link(last, apart=spare[:, 0:1])
                        stats(link, lambda t: R[0][:, t * P:(t + 1) * P], a2_st, a2_mv, a2_ve, 1e-5, ln2_var)
                    else:
                        last.then_inc(yn_ready, 1)
                if l == 0:
                    if j == 6:
                        dve.wait_ge(ln2_rstd, ka)
                        normalise(R[0], lambda t: R[0][:, t * P:(t + 1) * P], a2_mv, a2_rs).then_inc(yn_ready, 1)
                    if j == 9:
                        dve.wait_ge(proj_used, 5 * ka - 4)
                        link(dve.tensor_scalar(R[1], R[0], cols0[:, 5:6], cols0[:, 7:8], ALU.mult, ALU.add))
                        dve.tensor_scalar(R[0], R[0], cols0[:, 6:7], cols0[:, 8:9], ALU.mult, ALU.add).then_inc(qk_ready, 1)
                    if j in (13, 14):
                        q = j - 13
                        dve.wait_ge(av_ready, 2 * ka - 1 + q)
                        g = tiles(region[:, 2 * NT:4 * NT], NT)[:, :, q * SEQ:(q + 1) * SEQ]
                        dve.tensor_tensor(g, tiles(S[1 - q][:, :], SEQ), g, ALU.mult).then_inc(og_ready, 1)
                    if j == 15:
                        dve.wait_ge(ao_ready, ka)
                        dve.tensor_tensor(xs(X, b), xs(X, b), S[1][:, :], ALU.add).then_inc(x_done, 1)
                        assert link.n == LINKS_A[0], link.n
                else:
                    if j in (9, 10):
                        q = j - 9
                        dve.wait_ge(qkv_ready, 2 * ka - 1 + q)
                        dve.tensor_scalar(tiles(R[2][:, q * SEQ:(q + 1) * SEQ]), tiles(S[q][:, :], 2 * P)[:, :, 0:P], 0.0, None,
                                          ALU.min).then_inc(min_ready, 1)
                    if j == 12:
                        dve.wait_ge(exp_ready, ka)
                        for q in range(2):
                            last = dve.scalar_tensor_tensor(tiles(R[0][:, q * SEQ:(q + 1) * SEQ]), tiles(S[q][:, :], 2 * P)[:, :, 0:P],
                                                            0.0, tiles(R[2][:, q * SEQ:(q + 1) * SEQ]), ALU.max, ALU.add)
                        last.then_inc(phi_ready, 1)
                    if j == 14:
                        dve.wait_ge(kcum_ready, ka)
                        dve.tensor_tensor(tiles(kden[:, :], 64), tiles(S[0][:, 0:TB * 64], 64), tiles(R[0])[:, :, 0:64], ALU.mult).then_inc(den_read, 1)
                        dve.wait_ge(den_read, ka)
                        link(dve.tensor_reduce(den[:, :], kden[:, :].rearrange("p (a f) -> p a f", f=F), AX.X, ALU.add))
                        link(dve.tensor_scalar(den[:, :], den[:, :], 1e-6, None, ALU.add))
                        link(dve.reciprocal(rden[:, :], den[:, :]))
                    if j in (15, 16, 17, 18):
                        t = j - 15
                        dve.wait_ge(cum_ready, 4 * ka - 3 + t)
                        qq = R[0][:, t * P:t * P + 64].rearrange("p (h f) -> p h f", f=F)
                        dve.tensor_tensor(R[2].rearrange("p (h f g) -> p h f g", f=F, g=G),
                                          S[(t + 1) % 2][:, :].rearrange("p (h f g) -> p h f g", f=F, g=G),
                                          qq.unsqueeze(3).to_broadcast([P, HEADS, F, G]), ALU.mult).then_inc(cum_used, 1)
                        dve.wait_ge(cum_used, 4 * ka - 3 + t)
                        link(dve.tensor_reduce(xT[:, t * P:(t + 1) * P].rearrange("p (h g) -> p h g", g=G),
                                               R[2].rearrange("p (h f g) -> p h g f", f=F, g=G), AX.X, ALU.add))
                    if j == 19:
                        o = xT[:, :].rearrange("p (a g) -> p a g", g=G)
                        dve.tensor_tensor(o, o, over(rden[:, :], G), ALU.mult).then_inc(att_ready, 1)
                    if j == 23:
                        dve.wait_ge(ao_ready, NB + ka)
                        assert link.n == LINKS_A[1], link.n
                        dve.tensor_tensor(xs(X, b), xs(X, b), S[0][:, :], ALU.add).then_inc(x_done, 1)

            def sides(s, b, j, state):
                sa, ba = side_after(s, b)
                if sa >= 0:
                    if sa in (0, 2) and j == 0:
                        base = ba * LINKS_A[0] if sa == 0 else NB * LINKS_A[0] + ba * LINKS_A[1]
                        state["alink"] = Links(dve, a_link, base)
                    after_stage(sa, ba, j, state.get("alink"))
                if sa in (0, 2):
                    att_after(sa // 2, sa, ba, j, ba + 1, state["alink"])
                sb_, bb = side_before(s, b)
                if 0 <= sb_ < 3:
                    k = NB * (sb_ + 1) + bb + 1
                    if j == 0:
                        after_apart(dve, spare[:, 0:1], x_done, k - NB)
                    before(layer[sb_ + 1], j, k, bb, state)

            def prologue(b):
                state = {}
                for j in range(16):
                    before(0, j, b + 1, b, state)
            dve.wait_ge(x_loaded, 16 * NB)
            dve.wait_ge(small_loaded, 16 * 12)
            dve.wait_ge(consts, 5)
            prologue(0)
            with dve.Fori(1, NB) as b:
                prologue(b)
            for n in range(len(pieces0)):
                split_lo_piece(n)
            done = [len(pieces0)]

            def to_lo(n, j, rows):
                dve.wait_ge(hi_done, n + 1)
                ring = slice((j % RING) * NT, (j % RING + 1) * NT)
                dve.tensor_tensor(hL[0:rows, ring], hid[0:rows, (j % 2) * NT:(j % 2 + 1) * NT], hH[0:rows, ring].bitcast(F32),
                                  ALU.subtract).then_inc(lo_done, 1)

            def body(s, b):
                ex = experts[layer[s]]
                n = step_of(s, b)
                state = {}
                for j in range(steps[s]):
                    rows = ex.rows[j % ex.chunks]
                    dve.wait_ge(silu_done, n + j + 1)
                    after(dve, lo_done, n + j - 1)
                    half = slice((j % 2) * NT, (j % 2 + 1) * NT)
                    dve.tensor_tensor(hid[0:rows, half], UG[j % 2][0:rows, 0:NT], sg[0:rows, half], ALU.mult).then_inc(hid_done, 1)
                    if j:
                        to_lo(n + j - 1, j - 1, ex.rows[(j - 1) % ex.chunks])
                    elif prev_layer(s, b) is not None:
                        to_lo(n - 1, steps[side_after(s, b)[0]] - 1, experts[prev_layer(s, b)].rows[-1])
                    if s == 0 and isinstance(b, int) and b == 0:
                        for _ in splits_of_step(j):
                            split_lo_piece(done[0])
                            done[0] += 1
                    sides(s, b, j, state)

            each_body(dve, body)
            to_lo(first_step[4] - 1, steps[3] - 1, experts[1].rows[-1])
            sides(4, 0, 3, {})

        @block.tensor
        def _(pe):
            def before(l, j, k):
                if j == 7:
                    pe.wait_ge(z_ready, k)
                    after(pe, wT_used, k - 1)
                    for t in range(TB):
                        last = pe.transpose(S[2][:, t * P:(t + 1) * P], Z[:, t * P:(t + 1) * P], ident[:, :])
                    last.then_inc(zT_ready, 1)
                if j == 9:
                    pe.wait_ge(xh_ready, k)
                    for t in range(TB):
                        last = pe.matmul(S[2][:, t * E:(t + 1) * E], zT[:, t * P:(t + 1) * P], wr[:, l * E:(l + 1) * E],
                                         start=True, stop=True)
                    last.then_inc(score_ready, 1)
                if j == 14:
                    pe.wait_ge(w_ready, k)
                    for t in range(TB):
                        last = pe.transpose(S[2][0:E, t * P:(t + 1) * P], wt[:, t * E:(t + 1) * E], ident[:, :])
                    last.then_inc(wT_ready, 1)

            def after_stage(s, b, j):
                if j == 3:
                    m = NB * s + b
                    pe.wait_ge(accT, m + 1)
                    after(pe, x_done, m)
                    for t in range(TB):
                        last = pe.transpose(S[0][:, t * P:(t + 1) * P], R[3][:, t * P:(t + 1) * P], ident[:, :])
                    last.then_inc(acc_tok, 1)

            def att_after(l, j, ka):
                if j == (7 if l == 0 else 6):
                    pe.wait_ge(yn_ready, ka + 4 * l)
                    for t in range(TB):
                        last = pe.transpose(S[1][:, t * P:(t + 1) * P], R[0][:, t * P:(t + 1) * P], ident[:, :])
                    last.then_inc(ynT_ready, 1)
                if l == 0:
                    if j == 8:
                        pe.wait_ge(xT_ready, ka)
                        pe.matmul(S[0][:, :], w_qk[:, :], xT[:, :], start=True, stop=True).then_inc(proj_ready, 1)
                    if j in (8, 9):
                        c = j - 8
                        if c:
                            pe.wait_ge(proj_used, 5 * ka - 4)
                        pe.matmul(S[1 - c][:, :], w_hid[:, HID + c * P:HID + (c + 1) * P], xT[:, :], start=True, stop=True).then_inc(proj_ready, 1)
                    if j in (9, 10):
                        q = j - 9
                        pe.wait_ge(proj_used, 5 * ka - 3 + q)
                        for t in range(2):
                            o = S[1 - q][:, t * HID:(t + 1) * HID]
                            pe.matmul(o, xT[:, (2 * q + t) * P:(2 * q + t + 1) * P], w_hid[:, 0:HID], start=True, stop=False)
                            last = pe.matmul(o, ones[0:1, :], brow0[:, :], start=False, stop=True)
                        last.then_inc(proj_ready, 1)
                    if j in (10, 11):
                        q = j - 10
                        pe.wait_ge(proj_used, 5 * ka - 1 + q)
                        pe.wait_ge(qk_ready, ka)
                        for t in range(2):
                            last = pe.matmul(S[1 - q][:, t * SEQ:(t + 1) * SEQ], R[0][:, q * SEQ + t * P:q * SEQ + (t + 1) * P],
                                             R[1][:, q * SEQ:(q + 1) * SEQ], start=True, stop=True)
                        last.then_inc(sim_ready, 1)
                    if j in (12, 13):
                        q = j - 12
                        pe.wait_ge(sq_ready, 2 * ka - 1 + q)
                        for c in range(2):
                            for t in range(2):
                                last = pe.matmul(S[1 - q][:, c * SEQ:(c + 1) * SEQ], R[4 + q][:, t * HID + c * P:t * HID + (c + 1) * P],
                                                 R[6 + q][:, t * SEQ:(t + 1) * SEQ], start=(t == 0), stop=(t == 1))
                        last.then_inc(av_ready, 1)
                    if j == 15:
                        pe.wait_ge(og_ready, 2 * ka)
                        for t in range(TB):
                            o = S[1][:, t * P:(t + 1) * P]
                            for c in range(2):
                                pe.matmul(o, R[2 + c][:, t * P:(t + 1) * P], w_o0[:, c * P:(c + 1) * P], start=(c == 0), stop=False)
                            last = pe.matmul(o, ones[0:1, :], orow0[:, :], start=False, stop=True)
                        last.then_inc(ao_ready, 1)
                else:
                    if j in (8, 9):
                        q = j - 8
                        pe.wait_ge(xT_ready, NB + ka)
                        for t in range(2):
                            o = S[q][:, t * 2 * P:(t + 1) * 2 * P]
                            pe.matmul(o, xT[:, (2 * q + t) * P:(2 * q + t + 1) * P], w_qkv[:, :], start=True, stop=False)
                            last = pe.matmul(o, ones[0:1, :], brow1[:, :], start=False, stop=True)
                        last.then_inc(qkv_ready, 1)
                    if j == 13:
                        pe.wait_ge(phi_ready, ka)
                        for t in range(TB):
                            o = S[0][:, t * 64:(t + 1) * 64]
                            last = pe.matmul(o, tri[:, :], R[0][:, t * P + 64:(t + 1) * P], start=True, stop=(t % 2 == 0))
                            if t % 2:
                                last = pe.matmul(o, ones[:, :], R[0][:, (t - 1) * P + 64:t * P], start=False, stop=True)
                        last.then_inc(kcum_ready, 1)
                    if j in (14, 15, 16, 17):
                        t = j - 14
                        pe.wait_ge(kv_ready, 4 * ka - 3 + t)
                        if t == 0:
                            pe.wait_ge(v_ready, 2 * ka)
                        if t == 1:
                            pe.wait_ge(den_read, ka)
                        if t >= 2:
                            pe.wait_ge(cum_used, 4 * ka - 5 + t)
                        o = S[(t + 1) % 2][:, :]
                        last = pe.matmul(o, tri[:, :], R[3 + t], start=True, stop=(t % 2 == 0))
                        if t % 2:
                            last = pe.matmul(o, ones[:, :], R[2 + t], start=False, stop=True)
                        last.then_inc(cum_ready, 1)
                    if j == 20:
                        pe.wait_ge(att_ready, ka)
                        for t in range(TB):
                            last = pe.transpose(S[1][:, t * P:(t + 1) * P], xT[:, t * P:(t + 1) * P], ident[:, :])
                        last.then_inc(attT_ready, 1)
                    if j == 22:
                        pe.wait_ge(attT_used, ka)
                        for t in range(TB):
                            o = S[0][:, t * P:(t + 1) * P]
                            pe.matmul(o, R[1][:, t * P:(t + 1) * P], w_o1[:, :], start=True, stop=False)
                            last = pe.matmul(o, ones[0:1, :], orow1[:, :], start=False, stop=True)
                        last.then_inc(ao_ready, 1)

            def sides(s, b, j):
                sa, ba = side_after(s, b)
                if sa >= 0:
                    after_stage(sa, ba, j)
                if sa in (0, 2):
                    att_after(sa // 2, j, ba + 1)
                sb_, bb = side_before(s, b)
                if 0 <= sb_ < 3:
                    before(layer[sb_ + 1], j, NB * (sb_ + 1) + bb + 1)

            pe.wait_ge(consts, 5)
            pe.wait_ge(small_loaded, 16 * 12)

            def prologue(k):
                for j in range(16):
                    before(0, j, k)
            prologue(1)
            with pe.Fori(2, NB + 1) as k:
                prologue(k)

            def down(l, n, j):
                ex = experts[l]
                c = j % ex.chunks
                rows, at = ex.rows[c], ex.down_at(j // ex.chunks, c)
                ring = slice((j % RING) * NT, (j % RING + 1) * NT)
                pe.wait_ge(lo_done, n + 1)
                if j == 0:
                    after(pe, accT, block_of[0])
                wh, wl = downH[l][0:rows, at:at + P], downL[l][0:rows, at:at + P]
                hh, hl = hH[0:rows, ring], hL[0:rows, ring]
                pe.matmul(ACC[:, :], wh, hh, start=(j == 0), stop=False)
                pe.matmul(ACC[:, :], wh, hl, start=False, stop=False)
                pe.matmul(ACC[:, :], wl, hh, start=False, stop=(j == ex.steps - 1)).then_inc(down_done, 1)

            block_of = [0]

            def body(s, b):
                l = layer[s]
                ex = experts[l]
                n = step_of(s, b)
                block_of[0] = NB * s + b
                for j in range(steps[s]):
                    e, c = j // ex.chunks, j % ex.chunks
                    rows, at = ex.rows[c], ex.up_at(e, c)
                    if j == 0:
                        pe.wait_ge(xl_ready, NB * s + b + 1)
                    if s == 0 and isinstance(b, int) and b == 0:
                        pe.wait_ge(split_lo, at // NT + 1)
                    if s == 2 and isinstance(b, int) and b == 0 and j == 0:
                        pe.wait_ge(split_lo, len(split_all))
                    after(pe, hid_done, n + j - 1)
                    for half in range(2):
                        cols = slice(at + half * rows, at + (half + 1) * rows)
                        o = UG[j % 2][0:rows, half * NT:(half + 1) * NT]
                        pe.matmul(o, upH[l][:, cols], xs(xH, b), start=True, stop=False)
                        pe.matmul(o, upH[l][:, cols], xs(xL, b), start=False, stop=False)
                        last = pe.matmul(o, upL[l][:, cols], xs(xH, b), start=False, stop=True)
                    last.then_inc(up_done, 1)
                    if j >= LAG:
                        if s == 0 and isinstance(b, int) and b == 0 and j == LAG:
                            pe.wait_ge(split_lo, len(pieces0))
                        down(l, n + j - LAG, j - LAG)
                    elif prev_layer(s, b) is not None:
                        down(prev_layer(s, b), n + j - LAG, steps[side_after(s, b)[0]] + j - LAG)
                    sides(s, b, j)

            each_body(pe, body)
            for j in range(LAG):
                down(1, first_step[4] + j - LAG, steps[3] + j - LAG)
            sides(4, 0, 3)


_OUTS = [((8, 256, 128), "float32")]


def kernel(**inputs):
    import numpy as np
    import concourse.bacc as bacc
    from concourse.bass_utils import run_bass_kernel_spmd

    g = {k: np.asarray(v) for k, v in inputs.items()}

    def up(w, hidden):
        e = w.shape[0]
        parts = []
        for c in range(0, hidden, P):
            n = min(P, hidden - c)
            parts += [w[:, c:c + n, :], w[:, hidden + c:hidden + c + n, :]]
        return np.concatenate(parts, axis=1).transpose(2, 0, 1).reshape(P, e * 2 * hidden)

    def down(w, first, last, rows):
        n = (last - first) // rows
        return w[:, :, first:last].reshape(w.shape[0], P, n, rows).transpose(3, 2, 0, 1).reshape(rows, n * w.shape[0] * P)

    def cols(*vectors):
        return np.stack(vectors, axis=1)

    bh, osw, osb = g["L0_attn_b_hidden"], g["L0_attn_os_weight"], g["L0_attn_os_bias"]
    w1d = g["L1_ffn_w_down"]
    arrays = {
        "x": g["L0_attn_x"].reshape(-1, P),
        "up0": up(g["L0_ffn_w_up"], 256),
        "down0": down(g["L0_ffn_w_down"], 0, 256, P),
        "up1": up(g["L1_ffn_w_up"], 352),
        "down1a": down(w1d, 0, 256, P),
        "down1b": down(w1d, 256, 352, 96),
        "router": np.concatenate([g["L0_ffn_w_router"].T, g["L1_ffn_w_router"].T], axis=1),
        "norm": cols(g["L0_ffn_norm_scale"], g["L1_ffn_norm_scale"]),
        "att0_w": g["L0_attn_W_hidden"],
        "att0_qk": g["L0_attn_W_qk"],
        "att0_out": g["L0_attn_W_out"].reshape(2, P, P).transpose(1, 0, 2).reshape(P, 2 * P),
        "att0_cols": cols(g["L0_attn_ln_scale"], g["L0_attn_ln_bias"], g["L0_attn_b_qk"], bh[HID:HID + P], bh[HID + P:],
                          osw[0], osw[1], osb[0], osb[1]),
        "att0_brow": bh[None, :HID],
        "att0_orow": g["L0_attn_b_out"][None, :],
        "att1_w": np.concatenate([g["L1_attn_wq"], g["L1_attn_wk"], g["L1_attn_wv"]], axis=1),
        "att1_brow": np.concatenate([g["L1_attn_bq"], g["L1_attn_bk"], g["L1_attn_bv"]])[None, :],
        "att1_out": g["L1_attn_wo"],
        "att1_orow": g["L1_attn_bo"][None, :],
    }
    nc = bacc.Bacc("TRN2", target_bir_lowering=False, num_devices=1)
    feed, args = {}, []
    for name, a in arrays.items():
        a = np.ascontiguousarray(a)
        feed[f"in_{name}"] = a
        args.append(nc.dram_tensor(f"in_{name}", a.shape, mybir.dt.from_np(a.dtype), kind="ExternalInput").ap())
    args.append(nc.dram_tensor("out", [2048, P], F32, kind="ExternalOutput").ap())
    macaron(nc, *args)
    r = run_bass_kernel_spmd(nc, [feed], core_ids=[0])
    return r.results[0]["out"].reshape(8, 256, 128)
```

```python
import concourse.bass as bass
from concourse import mybir
from contextlib import ExitStack

F32 = mybir.dt.float32
F32R = mybir.dt.float32r
ALU = mybir.AluOpType
ACT = mybir.ActivationFunctionType
AX = mybir.AxisListType

P = 128
NT = 512
TB = NT // P
E = 8
SEQ = 256
HID = 256
HEADS, F, G = 16, 4, 8
LAG = 4
RING = 4
SPLIT_LAG = 2
BIAS = 2 * HID + 2 * P
HUGE = 3.0e38


class Experts:

    def __init__(self, hidden):
        self.hidden = hidden
        self.rows = [min(P, hidden - c * P) for c in range((hidden + P - 1) // P)]
        self.chunks = len(self.rows)
        self.steps = E * self.chunks

    def up_at(self, e, c):
        return e * 2 * self.hidden + c * 2 * P

    def down_at(self, e, c):
        return (c * E + e) * P


def after(eng, sem, count):
    if not (isinstance(count, int) and count <= 0):
        eng.wait_ge(sem, count)


def after_apart(eng, cell, sem, count):
    eng.wait_ge(sem, count)
    if not isinstance(count, int):
        eng.memset(cell, 0.0)


class Links:

    def __init__(self, eng, sem, base):
        self.eng, self.sem, self.base, self.n = eng, sem, base, 0

    def __call__(self, ins, apart=None):
        self.n += 1
        ins.then_inc(self.sem, 1)
        if apart is None:
            self.eng.wait_ge(self.sem, self.base + self.n)
        else:
            after_apart(self.eng, apart, self.sem, self.base + self.n)


def macaron(nc, x, up0, down0, up1, down1a, down1b, router, norm, att0_w, att0_qk, att0_out, att0_cols,
            att1_w, att1_out, bias_rows, out):
    experts = [Experts(256), Experts(352)]
    layer = [0, 0, 1, 1]
    NB = x.shape[0] // NT
    steps = [experts[l].steps for l in layer]
    first_step = [NB * sum(steps[:s]) for s in range(5)]
    ctx = ExitStack()
    with ctx:
        def sb(name, cols, dt=F32, rows=P):
            return ctx.enter_context(nc.sbuf_tensor(name, [rows, cols], dt))

        def sem(name):
            return ctx.enter_context(nc.semaphore(name))

        upH = [sb(f"up{l}_hi", 2 * experts[l].hidden * E, F32R) for l in range(2)]
        upL = [sb(f"up{l}_lo", 2 * experts[l].hidden * E, F32R) for l in range(2)]
        downH = [sb(f"down{l}_hi", experts[l].chunks * E * P, F32R) for l in range(2)]
        downL = [sb(f"down{l}_lo", experts[l].chunks * E * P, F32R) for l in range(2)]
        X = sb("x_res", NB * NT)
        xH = sb("xn_hi", NB * NT, F32R)
        xL = sb("xn_lo", NB * NT, F32R)
        hid = sb("hidden", RING * NT)
        hH = sb("hidden_hi", RING * NT, F32R)
        hL = sb("hidden_lo", RING * NT, F32R)
        wtok = sb("token_weights", 2 * NT)
        region = sb("attention", 8 * NT)
        R = [region[:, i * NT:(i + 1) * NT] for i in range(8)]
        xT = sb("attn_xT", NT)
        spare = sb("spare", 2)
        a_st = sb("a_stats", TB * 6)
        a_mv = sb("a_meanvar", TB * 2)
        a_ve = sb("a_var", TB)
        a_rs = sb("a_rstd", TB)
        kden = sb("k_den", TB * 64)
        den = sb("den", TB * HEADS)
        rden = sb("rden", TB * HEADS)
        Z = sb("rms_out", NT)
        zT = Z
        stage2 = [sb(f"weight_stage{i}", NT) for i in range(2)]
        b_st = sb("b_stats", TB * 6)
        b_mv = sb("b_meanvar", TB * 2)
        b_ve = sb("b_var", 2 * TB)
        b_rs = sb("b_rstd", 2 * TB)
        b_mul = sb("b_skip_mul", TB)
        b_add = sb("b_skip_add", TB)
        m1 = sb("top1", TB)
        m2 = sb("top2", TB)
        pm = sb("pick", TB)
        e1 = sb("is_max", TB * E)
        oh1 = sb("first", TB * E)
        oh2 = sb("second", TB * E)
        rest = sb("rest", TB * E)
        th = sb("tanh", TB * E)
        thn = sb("one_minus", TB * E)
        w1 = sb("w_first", TB)
        w2 = sb("w_second", TB)
        wt = sb("w_tok", TB * E)
        wtT = sb("w_tokT", NT, rows=E)
        ident = sb("ident", P)
        ones = sb("ones", P)
        tri = sb("tri", P)
        mhalf = sb("minus_half", 2 * TB)
        row1 = sb("minus_row1", 1, rows=2)
        onesR = sb("ones_r", P, F32R, rows=2)
        brows = sb("bias_rows", BIAS, F32R, rows=2)
        bias_v, bias_o0, bias_qkv, bias_o1 = (brows[:, a:z] for a, z in ((0, HID), (HID, HID + P), (HID + P, 2 * HID + P), (2 * HID + P, BIAS)))
        prio = sb("priority", TB * E)
        wr = sb("router", 2 * E)
        wn = sb("norm", 2)
        w_hid = sb("a0_hidden", 2 * HID)
        w_qk = sb("a0_qk", P)
        w_o0 = sb("a0_out", 2 * P)
        cols0 = sb("a0_cols", 9)
        w_qkv = sb("a1_qkv", 2 * P)
        w_o1 = sb("a1_out", P)

        UG = [ctx.enter_context(nc.psum_tensor(f"up_gate{i}", [P, 2 * NT], F32)) for i in range(2)]
        ACC = ctx.enter_context(nc.psum_tensor("acc", [P, NT], F32))
        S = [ctx.enter_context(nc.psum_tensor(f"side{i}", [P, NT], F32)) for i in range(3)]
        WD = nc.dram_tensor("token_weights_dram", [NB * E, NT], F32, kind="Internal").ap()

        x_loaded = sem("x_loaded")
        small_loaded = sem("small_loaded")
        norm_loaded = sem("norm_loaded")
        x_rest_loaded = sem("x_rest_loaded")
        x1_loaded = sem("x1_loaded")
        stage_loaded = [sem(f"stage_loaded{i}") for i in range(6)]
        wtok_loaded = [sem(f"wtok_loaded{i}") for i in range(2)]
        bias_hi, bias_split = sem("bias_hi"), sem("bias_split")
        wd_stored = sem("wd_stored")
        out_stored = sem("out_stored")
        consts = sem("consts")
        const_base = sem("const_base")
        split_hi = sem("split_hi")
        split_lo0, split_lo1 = sem("split_lo0"), sem("split_lo1")
        up_done = sem("up_done")
        silu_done = sem("silu_done")
        hid_done = sem("hid_done")
        scaled = sem("scaled")
        hi_done = sem("hi_done")
        lo_done = sem("lo_done")
        down_done = sem("down_done")
        accT = sem("acc_evacuated")
        acc_tok = sem("acc_token_major")
        x_done = sem("x_done")
        ln1_var, ln1_rstd = sem("ln1_var"), sem("ln1_rstd")
        yn_ready, ynT_ready, xT_ready = sem("yn_ready"), sem("ynT_ready"), sem("xT_ready")
        proj_ready, proj_used = sem("proj_ready"), sem("proj_used")
        qk_ready, sim_ready, relu_ready, sq_ready = sem("qk_ready"), sem("sim_ready"), sem("relu_ready"), sem("sq_ready")
        av_ready, og_ready, ao_ready = sem("av_ready"), sem("og_ready"), sem("ao_ready")
        qkv_ready, min_ready, v_ready, exp_ready = sem("qkv_ready"), sem("min_ready"), sem("v_ready"), sem("exp_ready")
        phi_ready, kv_ready, kcum_ready, den_read = sem("phi_ready"), sem("kv_ready"), sem("kcum_ready"), sem("den_read")
        cum_ready, cum_used = sem("cum_ready"), sem("cum_used")
        att_ready, attT_ready, attT_used = sem("att_ready"), sem("attT_ready"), sem("attT_used")
        a_link = sem("a_link")
        b_var, b_rstd, skip_ready = sem("b_var"), sem("b_rstd"), sem("skip_ready")
        z_ready, zT_ready, zT_used, xh_ready = sem("z_ready"), sem("zT_ready"), sem("zT_used"), sem("xh_ready")
        score_ready, d_ready, th_ready = sem("score_ready"), sem("d_ready"), sem("th_ready")
        w_ready, wT_ready, wT_used, xl_ready = sem("w_ready"), sem("wT_ready"), sem("wT_used"), sem("xl_ready")
        b_link = sem("b_link")

        BIAS_AT = 12
        BSTEPS = 16
        LINKS_B = [20, 23]
        LINKS_A = [5, 10]

        def in_ring(t, j, rows):
            return t[0:rows, (j % RING) * NT:(j % RING + 1) * NT]

        def pieces(l):
            found = []
            sources = [(up0, upH[0], upL[0], 0, P), (down0, downH[0], downL[0], 0, P)] if l == 0 else \
                [(up1, upH[1], upL[1], 0, P), (down1a, downH[1], downL[1], 0, P),
                 (down1b, downH[1], downL[1], 2 * E * P, experts[1].rows[-1])]
            for src, hi, lo, at, rows in sources:
                for c in range(0, src.shape[1], NT):
                    found.append((src[:, c:c + NT], hi[0:rows, at + c:at + c + NT], lo[0:rows, at + c:at + c + NT], rows))
            return found

        pieces0 = pieces(0)
        up_piece = {0: 0, 1: 1, 2: 4, 3: 5, 4: 6, 5: 8, 6: 10, 7: 11}
        down_piece = {(0, 0): 2, (1, 0): 3, (0, 1): 7, (1, 1): 9}
        ordered = {n: pieces0[e] for e, n in up_piece.items()}
        ordered.update({n: pieces0[E + 2 * c + h] for (c, h), n in down_piece.items()})
        pieces0 = [ordered[n] for n in range(len(ordered))]
        pieces1 = pieces(1)
        split_all = pieces0 + pieces1

        HI_BEFORE, HI_STEP = 5, 0
        LO_BEFORE, LO_STEP = 7, 2
        LO_FIRST = 5
        LOAD_BEFORE = 10

        def piece_at(before, first, s, b, j):
            n = before + j - first
            return n if s == 0 and isinstance(b, int) and b == 0 and j >= first and n < len(pieces0) else None

        split_steps = {(0, 1): (0, 2, 12, 14), (1, 0): (0, 2, 12, 14), (1, 1): (0, 1, 3, 5, 7, 9, 11, 13, 15)}
        assert sum(map(len, split_steps.values())) == len(pieces1)

        def splits_at(s, b, j):
            return isinstance(b, int) and j in split_steps.get((s, b), ())

        def staging(n):
            n0 = len(pieces0)
            if n < n0:
                return R[n % 4], stage_loaded[n % 4], 16 * (n // 4 + 1), split_lo0, n - 3
            return stage2[n % 2], stage_loaded[4 + n % 2], 16 * ((n - n0) // 2 + 1), split_lo1, n - n0 - 1

        def each_body(eng, body):
            for s in range(4):
                body(s, 0)
                body(s, 1)
                with eng.Fori(2, NB) as b:
                    body(s, b)

        def side_after(s, b):
            return (s, b - 1) if not (isinstance(b, int) and b == 0) else (s - 1, NB - 1)

        def side_before(s, b):
            return (s, b - 2) if not (isinstance(b, int) and b < 2) else (s - 1, b + NB - 2)

        TWO_IN_ONE = ((0, 1), (2, 3), (4, 5), (6, 7), (8, 9), (10, 11), (12,), (14, 15))
        TAIL = 14
        TAIL_AT = 0

        def first_prep(s, b, j):
            if s or not isinstance(b, int) or b > 1:
                return []
            if b == 1:
                return [(3, (j,))]
            n = len(TWO_IN_ONE)
            tail = [(0, tuple(range(TAIL, BSTEPS)))] if j == TAIL_AT else []
            return tail + [(1 + j // n, TWO_IN_ONE[j % n])]

        def step_of(s, b):
            return first_step[s] + (b * steps[s] if s < 4 else 0)

        def prev_layer(s, b):
            return layer[side_after(s, b)[0]] if side_after(s, b)[0] >= 0 else None

        def to_split(split, s, b, j):
            if j >= SPLIT_LAG:
                ex, j_ = experts[layer[s]], j - SPLIT_LAG
            elif prev_layer(s, b) is not None:
                ex = experts[prev_layer(s, b)]
                j_ = ex.steps + j - SPLIT_LAG
            else:
                return
            split(step_of(s, b) + j - SPLIT_LAG, j_, ex.rows[j_ % ex.chunks])

        def xs(t, b, at=0, n=NT):
            if isinstance(b, int):
                return t[:, b * NT + at:b * NT + at + n]
            return t[:, bass.ds(b * NT + at, n)]

        def tiles(ap, cols=P):
            return ap.rearrange("p (t c) -> p t c", c=cols)

        def over(ap, n):
            return ap.unsqueeze(2).to_broadcast([ap.shape[0], ap.shape[1], n])

        block = ctx.enter_context(nc.Block())

        @block.sync
        def _(sp):
            def load_x(b, loaded):
                sp.dma_start(tiles(xs(X, b)), x[b * NT:(b + 1) * NT, :].rearrange("(t p) d -> p t d", p=P)).then_inc(loaded, 16)

            def load_piece(n):
                src, _, _, rows = split_all[n]
                buf, loaded, _, split_lo, gone = staging(n)
                after(sp, split_lo, gone)
                sp.dma_start(buf[0:rows, :], src).then_inc(loaded, 16)

            load_x(0, x_loaded)
            sp.dma_start(wn[:, :], norm).then_inc(norm_loaded, 16)
            sp.dma_start(wr[:, :], router).then_inc(norm_loaded, 16)
            for n in range(LOAD_BEFORE):
                load_piece(n)
                if n == 1:
                    load_x(1, x1_loaded)
                if n == 5:
                    for b in range(2, NB):
                        load_x(b, x_rest_loaded)

            def load_small():
                small = ((w_hid, att0_w), (w_qk, att0_qk), (w_o0, att0_out), (cols0, att0_cols), (w_qkv, att1_w), (w_o1, att1_out))
                for dst, src in small:
                    sp.dma_start(dst[:, :], src).then_inc(small_loaded, 16)
                sp.dma_start(region[0:2, 5 * NT:5 * NT + BIAS], bias_rows).then_inc(small_loaded, 16)

            def store_out(b):
                after(sp, x_done, 3 * NB + b + 1)
                rows = out[b * NT:(b + 1) * NT, :] if isinstance(b, int) else out[bass.ds(b * NT, NT), :]
                sp.dma_start(rows.rearrange("(t p) d -> p t d", p=P), tiles(xs(X, b))).then_inc(out_stored, 16)

            to_load = [LOAD_BEFORE]

            def body(s, b):
                ex = experts[layer[s]]
                m = NB * s + b
                after(sp, wd_stored, 16 * (m + 1))
                for e in range(E):
                    if e >= 2:
                        after(sp, scaled, step_of(s, b) + (e - 1) * ex.chunks)
                    elif prev_layer(s, b) is not None:
                        after(sp, scaled, step_of(s, b) - (1 - e) * experts[prev_layer(s, b)].chunks)
                    row = WD[b * E + e:b * E + e + 1, :] if isinstance(b, int) else WD[bass.ds(b * E + e, 1), :]
                    sp.dma_start(wtok[:, (e % 2) * NT:(e % 2 + 1) * NT], row.to_broadcast([P, NT])).then_inc(wtok_loaded[e % 2], 16)
                    if s == 0 and isinstance(b, int) and b == 0:
                        if e == 4:
                            load_small()
                        for _ in {1: range(1), 3: range(1), 5: range(2)}.get(e, ()):
                            load_piece(to_load[0])
                            to_load[0] += 1
                    if s < 2 and isinstance(b, int):
                        for j in range(e * ex.chunks, (e + 1) * ex.chunks):
                            if splits_at(s, b, j) and to_load[0] < len(split_all):
                                load_piece(to_load[0])
                                to_load[0] += 1
                if s == 3 and not (isinstance(b, int) and b == 0):
                    store_out(b - 1)

            each_body(sp, body)
            store_out(NB - 1)
            sp.wait_ge(out_stored, 16 * NB)

        @block.gpsimd
        def _(pool):
            pool.memset(ident[:, :], 0.0).then_inc(const_base, 1)
            pool.memset(tri[:, :], 1.0).then_inc(const_base, 1)
            pool.memset(ones[:, :], 1.0).then_inc(consts, 1)
            pool.memset(mhalf[:, :], -0.5).then_inc(consts, 1)
            for e in range(E):
                last = pool.memset(tiles(prio[:, :], E)[:, :, e:e + 1], float(E - e))
            last.then_inc(consts, 1)
            pool.memset(row1[:, :], -1.0).then_inc(const_base, 1)
            pool.wait_ge(const_base, 3)
            pool.affine_select(out=ident[:, :], in_=ident[:, :], compare_op=ALU.not_equal, fill=1.0, base=0,
                               pattern=[[-1, P]], channel_multiplier=1).then_inc(consts, 1)
            pool.affine_select(out=row1[:, :], in_=row1[:, :], compare_op=ALU.is_gt, fill=0.0, base=0,
                               pattern=[[0, 1]], channel_multiplier=1).then_inc(consts, 1)
            pool.affine_select(out=tri[:, :], in_=tri[:, :], compare_op=ALU.is_ge, fill=0.0, base=0,
                               pattern=[[1, P]], channel_multiplier=-1).then_inc(consts, 1)
            pool.wait_ge(consts, 6)

            def before(l, j, k, b):
                if j == 1:
                    pool.wait_ge(b_var, k)
                    pool.tensor_tensor(b_rs[:, :], b_ve[:, :], mhalf[:, :], ALU.pow).then_inc(b_rstd, 1)

            def att_after(l, j, ka):
                if j == 5:
                    pool.wait_ge(ln1_var, ka + 4 * l)
                    pool.tensor_tensor(a_rs[:, :], a_ve[:, :], mhalf[:, 0:TB], ALU.pow).then_inc(ln1_rstd, 1)
                if l == 1 and j in (13, 14, 15, 16):
                    t = j - 13
                    if t == 0:
                        pool.wait_ge(phi_ready, ka)
                    if t % 2 == 0:
                        pool.wait_ge(v_ready, 2 * ka - 1 + t // 2)
                    kk = R[0][:, t * P + 64:(t + 1) * P].rearrange("p (h f) -> p h f", f=F)
                    vv = R[1][:, t * P:(t + 1) * P].rearrange("p (h g) -> p h g", g=G)
                    pool.tensor_tensor(R[3 + t].rearrange("p (h f g) -> p h f g", f=F, g=G),
                                       kk.unsqueeze(3).to_broadcast([P, HEADS, F, G]),
                                       vv.unsqueeze(2).to_broadcast([P, HEADS, F, G]), ALU.mult).then_inc(kv_ready, 1)

            def sides(s, b, j):
                sa, ba = side_after(s, b)
                if sa in (0, 2):
                    att_after(sa // 2, j, ba + 1)
                sb_, bb = side_before(s, b)
                if 0 <= sb_ < 3:
                    before(layer[sb_ + 1], j, NB * (sb_ + 1) + bb + 1, bb)
                for blk, js in first_prep(s, b, j):
                    for j_ in js:
                        before(0, j_, blk + 1, blk)

            def split_lo_piece(n):
                _, hi, lo, rows = pieces0[n]
                pool.wait_ge(split_hi, n + 1)
                pool.tensor_tensor(lo, staging(n)[0][0:rows, :], hi.bitcast(F32), ALU.subtract).then_inc(split_lo0, 1)

            for j in range(TAIL):
                before(0, j, 1, 0)
            for n in range(LO_FIRST):
                split_lo_piece(n)

            def body(s, b):
                ex = experts[layer[s]]
                n = step_of(s, b)
                for j in range(steps[s]):
                    e, c = j // ex.chunks, j % ex.chunks
                    rows = ex.rows[c]
                    first = s == 0 and isinstance(b, int) and b == 0 and j == 0
                    if first:
                        sides(s, b, j)
                        for n_ in range(LO_FIRST, LO_BEFORE):
                            split_lo_piece(n_)
                    if c == 0:
                        pool.wait_ge(wtok_loaded[e % 2], 16 * (4 * (NB * s + b) + e // 2 + 1))
                    pool.wait_ge(hid_done, n + j + 1)
                    h = in_ring(hid, j, rows)
                    pool.tensor_tensor(h, h, wtok[0:rows, (e % 2) * NT:(e % 2 + 1) * NT], ALU.mult).then_inc(scaled, 1)
                    if piece_at(LO_BEFORE, LO_STEP, s, b, j) is not None:
                        split_lo_piece(piece_at(LO_BEFORE, LO_STEP, s, b, j))
                    if not first:
                        sides(s, b, j)

            each_body(pool, body)

        @block.scalar
        def _(act):
            def split_hi_piece(n):
                _, hi, _, rows = split_all[n]
                buf, loaded, value = staging(n)[:3]
                act.wait_ge(loaded, value)
                act.activation(hi, buf[0:rows, :], ACT.Copy).then_inc(split_hi, 1)

            def before(l, j, k, b):
                if j == 5:
                    act.wait_ge(zT_ready, k)
                    act.activation(zT[:, :], S[2][:, :], ACT.Copy, scale=wn[:, l:l + 1]).then_inc(zT_used, 1)
                    act.activation(xs(xH, b), S[2][:, :], ACT.Copy, scale=wn[:, l:l + 1]).then_inc(xh_ready, 1)
                if j == 10:
                    act.wait_ge(d_ready, k)
                    if l == 0:
                        act.activation(th[:, 0:TB], w1[:, :], ACT.Tanh, scale=0.5).then_inc(th_ready, 1)
                    else:
                        act.activation(th[:, :], rest[:, :], ACT.Tanh, scale=0.5).then_inc(th_ready, 1)
                if j == 15:
                    act.wait_ge(wT_ready, k)
                    after(act, wd_stored, 16 * (k - 1))
                    act.activation(wtT[:, :], S[2][0:E, :], ACT.Copy).then_inc(wT_used, 1)
                    act.wait_ge(wT_used, k)
                    rows = WD[b * E:(b + 1) * E, :] if isinstance(b, int) else WD[bass.ds(b * E, E), :]
                    act.dma_start(rows, wtT[:, :]).then_inc(wd_stored, 16)

            def after_stage(s, b, j):
                if j == LAG - 1:
                    m = NB * s + b
                    act.wait_ge(down_done, step_of(s, b) + steps[s])
                    after(act, x_done, m)
                    act.activation(R[3], ACC[:, :], ACT.Copy).then_inc(accT, 1)

            def att_after(l, j, ka):
                if j == 7:
                    act.wait_ge(ynT_ready, ka + 4 * l)
                    if l == 0:
                        act.activation(xT[:, :], S[1][:, :], ACT.Identity, scale=cols0[:, 0:1], bias=cols0[:, 1:2]).then_inc(xT_ready, 1)
                    else:
                        act.activation(xT[:, :], S[1][:, :], ACT.Copy).then_inc(xT_ready, 1)
                if l == 0:
                    for i in {8: (0, 1), 9: (2, 3), 10: (4,)}.get(j, ()):
                        act.wait_ge(proj_ready, 5 * ka - 4 + i)
                        dst, src, bias = ((R[0], S[0], cols0[:, 2:3]), (R[2], S[1], cols0[:, 3:4]), (R[3], S[0], cols0[:, 4:5]),
                                          (R[4], S[1], 0.0), (R[5], S[0], 0.0))[i]
                        act.activation(dst, src[:, :], ACT.Silu, bias=bias).then_inc(proj_used, 1)
                    if j in (11, 12):
                        q = j - 11
                        act.wait_ge(sim_ready, 2 * ka - 1 + q)
                        act.activation(R[6 + q], S[1 - q][:, :], ACT.Relu, scale=1.0 / SEQ).then_inc(relu_ready, 1)
                else:
                    if j in (10, 13):
                        q = (j - 10) // 3
                        if q == 0:
                            act.wait_ge(min_ready, 2 * ka - 1)
                        else:
                            act.wait_ge(phi_ready, ka)
                        act.activation(tiles(R[1][:, q * SEQ:(q + 1) * SEQ]), tiles(S[q][:, :], 2 * P)[:, :, P:2 * P], ACT.Copy).then_inc(v_ready, 1)
                    if j == 11:
                        act.wait_ge(min_ready, 2 * ka)
                        act.activation(R[2], R[2], ACT.Exp).then_inc(exp_ready, 1)
                    if j == 21:
                        act.wait_ge(attT_ready, ka)
                        act.activation(R[1], S[1][:, :], ACT.Copy).then_inc(attT_used, 1)

            def sides(s, b, j):
                sa, ba = side_after(s, b)
                if sa >= 0:
                    after_stage(sa, ba, j)
                if sa in (0, 2):
                    att_after(sa // 2, j, ba + 1)
                sb_, bb = side_before(s, b)
                if 0 <= sb_ < 3:
                    before(layer[sb_ + 1], j, NB * (sb_ + 1) + bb + 1, bb)
                for blk, js in first_prep(s, b, j):
                    for j_ in js:
                        before(0, j_, blk + 1, blk)
                if s == 0 and isinstance(b, int) and b == 0 and j == BIAS_AT:
                    act.activation(onesR[:, :], ones[0:2, :], ACT.Copy)
                    act.wait_ge(small_loaded, 16 * 7)
                    act.activation(brows[:, :], region[0:2, 5 * NT:5 * NT + BIAS], ACT.Copy).then_inc(bias_hi, 1)

            act.wait_ge(consts, 6)
            act.activation(th[:, 0:1], ones[:, 0:1], ACT.Silu)
            split_hi_piece(0)
            act.wait_ge(norm_loaded, 32)
            for j in range(TAIL):
                before(0, j, 1, 0)
                for n in {5: (1, 2), 10: range(3, HI_BEFORE)}.get(j, ()):
                    split_hi_piece(n)
            done = [len(pieces0)]

            def to_hi(n, j, rows):
                act.wait_ge(scaled, n + 1)
                after(act, down_done, n + 1 - RING)
                act.activation(in_ring(hH, j, rows), in_ring(hid, j, rows), ACT.Copy).then_inc(hi_done, 1)

            def body(s, b):
                ex = experts[layer[s]]
                n = step_of(s, b)
                for j in range(steps[s]):
                    rows = ex.rows[j % ex.chunks]
                    act.wait_ge(up_done, n + j + 1)
                    after(act, lo_done, n + j + 1 - RING)
                    act.activation(in_ring(hid, j, rows), UG[j % 2][0:rows, NT:2 * NT], ACT.Silu).then_inc(silu_done, 1)
                    first = (s == 0 and isinstance(b, int) and b == 0 and j < RING) or True
                    if first:
                        sides(s, b, j)
                    to_split(to_hi, s, b, j)
                    if piece_at(HI_BEFORE, HI_STEP, s, b, j) is not None:
                        split_hi_piece(piece_at(HI_BEFORE, HI_STEP, s, b, j))
                    if splits_at(s, b, j):
                        split_hi_piece(done[0])
                        done[0] += 1
                    if not first:
                        sides(s, b, j)

            each_body(act, body)
            for j in range(SPLIT_LAG):
                to_split(to_hi, 4, 0, j)
            sides(4, 0, LAG - 1)

        @block.vector
        def _(dve):
            def split_lo_piece(n):
                _, hi, lo, rows = split_all[n]
                dve.wait_ge(split_hi, n + 1)
                dve.tensor_tensor(lo, staging(n)[0][0:rows, :], hi.bitcast(F32), ALU.subtract).then_inc(split_lo1, 1)

            def stats(link, src, st, mv, ve, eps2, alone, done, first=0, part=(0, 1)):
                if 0 in part:
                    for t in range(first, TB):
                        last = dve.bn_stats(st[:, 6 * t:6 * t + 6], src(t))
                    link(last, apart=spare[:, 0:1])
                if 1 not in part:
                    return
                for t in range(TB):
                    last = dve.bn_aggr(mv[:, 2 * t:2 * t + 2], st[:, 6 * t:6 * t + 6])
                link(last)
                var = mv[:, 1:2 * TB:2]
                ins = dve.tensor_scalar(ve[:, 0:TB], var, 1e-5, None, ALU.add)
                if eps2 is not None:
                    link(ins)
                    both = ve[:, TB:2 * TB] if alone else ve[:, 0:TB]
                    ins = dve.scalar_tensor_tensor(both, ve[:, 0:TB], eps2, var, ALU.mult, ALU.add)
                ins.then_inc(done, 1)

            def normalise(dst, src, mv, rs):
                for t in range(TB):
                    last = dve.tensor_scalar(dst[:, t * P:(t + 1) * P], src(t), mv[:, 2 * t:2 * t + 1], rs[:, t:t + 1],
                                             ALU.subtract, ALU.mult)
                return last

            def before(l, j, k, b, state):
                if j == 0:
                    base = (k - 1) * LINKS_B[0] if l == 0 else 2 * NB * LINKS_B[0] + (k - 1 - 2 * NB) * LINKS_B[1]
                    state["link"] = Links(dve, b_link, base)
                    for t in range(2):
                        dve.bn_stats(b_st[:, 6 * t:6 * t + 6], xs(X, b, t * P, P))
                if j == 1:
                    stats(state["link"], lambda t: xs(X, b, t * P, P), b_st, b_mv, b_ve, 1e-6, True, b_var, first=2)
                link = state["link"]
                sc = tiles(S[2][:, 0:TB * E], E)
                v = lambda t: tiles(t[:, :], E)
                if j == 3:
                    dve.wait_ge(b_rstd, k)
                    normalise(Z, lambda t: xs(X, b, t * P, P), b_mv, b_rs[:, TB:2 * TB]).then_inc(z_ready, 1)
                if j == 4:
                    link(dve.tensor_scalar(b_mul[:, :], b_rs[:, 0:TB], 0.5, 1.0, ALU.mult, ALU.add))
                    dve.scalar_tensor_tensor(b_add[:, :], b_mv[:, 0:2 * TB:2], -0.5, b_rs[:, 0:TB], ALU.mult, ALU.mult).then_inc(skip_ready, 1)
                if j == 5:
                    dve.wait_ge(skip_ready, k)
                    for t in range(TB):
                        last = dve.tensor_scalar(xs(X, b, t * P, P), xs(X, b, t * P, P), b_mul[:, t:t + 1], b_add[:, t:t + 1],
                                                 ALU.mult, ALU.add)
                    link(last, apart=spare[:, 0:1])
                if j == 7:
                    dve.wait_ge(score_ready, k)
                    link(dve.tensor_reduce(m1[:, :], sc, AX.X, ALU.max))
                    link(dve.tensor_tensor(v(e1), sc, over(m1[:, :], E), ALU.is_equal))
                    link(dve.tensor_tensor(e1[:, :], e1[:, :], prio[:, :], ALU.mult))
                    link(dve.tensor_reduce(pm[:, :], v(e1), AX.X, ALU.max))
                if j == 8:
                    link(dve.tensor_tensor(v(oh1), v(e1), over(pm[:, :], E), ALU.is_equal))
                    link(dve.scalar_tensor_tensor(v(rest), v(oh1), -HUGE, sc, ALU.mult, ALU.add))
                    link(dve.tensor_reduce(m2[:, :], v(rest), AX.X, ALU.max))
                if j == 9:
                    if l == 0:
                        dve.tensor_tensor(w1[:, :], m1[:, :], m2[:, :], ALU.subtract).then_inc(d_ready, 1)
                    link(dve.tensor_tensor(v(e1), v(rest), over(m2[:, :], E), ALU.is_equal))
                    link(dve.tensor_tensor(e1[:, :], e1[:, :], prio[:, :], ALU.mult))
                    link(dve.tensor_reduce(pm[:, :], v(e1), AX.X, ALU.max))
                    if l == 1:
                        dve.tensor_tensor(v(rest), sc, over(m1[:, :], E), ALU.subtract).then_inc(d_ready, 1)
                if j == 10:
                    link(dve.tensor_tensor(v(oh2), v(e1), over(pm[:, :], E), ALU.is_equal))
                    if l == 1:
                        link(dve.tensor_tensor(oh1[:, :], oh1[:, :], oh2[:, :], ALU.add))
                if j == 6:
                    dve.wait_ge(xh_ready, k)
                    dve.tensor_tensor(xs(xL, b), zT[:, :], xs(xH, b).bitcast(F32), ALU.subtract).then_inc(xl_ready, 1)
                if j == 11:
                    dve.wait_ge(th_ready, k)
                    if l == 0:
                        link(dve.tensor_scalar(w1[:, :], th[:, 0:TB], 0.25, 0.25, ALU.mult, ALU.add))
                        link(dve.tensor_scalar(w2[:, :], th[:, 0:TB], -0.25, 0.25, ALU.mult, ALU.add))
                    else:
                        link(dve.tensor_scalar(thn[:, :], th[:, :], -1.0, 1.0, ALU.mult, ALU.add))
                        link(dve.reciprocal(thn[:, :], thn[:, :]))
                        link(dve.scalar_tensor_tensor(rest[:, :], th[:, :], 1.0, thn[:, :], ALU.add, ALU.mult))
                if j == 12:
                    if l == 0:
                        link(dve.tensor_tensor(v(oh1), v(oh1), over(w1[:, :], E), ALU.mult))
                        link(dve.tensor_tensor(v(oh2), v(oh2), over(w2[:, :], E), ALU.mult))
                        dve.tensor_tensor(wt[:, :], oh1[:, :], oh2[:, :], ALU.add).then_inc(w_ready, 1)
                    else:
                        link(dve.tensor_reduce(w1[:, :], v(rest), AX.X, ALU.add))
                        link(dve.reciprocal(w2[:, :], w1[:, :]))
                        link(dve.scalar_tensor_tensor(rest[:, :], rest[:, :], 0.5, oh1[:, :], ALU.mult, ALU.mult))
                        dve.tensor_tensor(v(wt), v(rest), over(w2[:, :], E), ALU.mult).then_inc(w_ready, 1)
                    assert link.n == LINKS_B[l], (l, link.n)

            def after_stage(s, b, j, link):
                if j == LAG:
                    m = NB * s + b
                    dve.wait_ge(acc_tok, m + 1)
                    ins = dve.tensor_tensor(xs(X, b), xs(X, b), S[0][:, :], ALU.add)
                    if s in (0, 2):
                        link(ins, apart=spare[:, 0:1])
                    else:
                        ins.then_inc(x_done, 1)

            def att_after(l, s, b, j, ka, link):
                if j in (LAG, LAG + 1):
                    stats(link, lambda t: xs(X, b, t * P, P), a_st, a_mv, a_ve, 1e-5 if l == 0 else None, False, ln1_var,
                          part=(j - LAG,))
                if j == 6:
                    dve.wait_ge(ln1_rstd, ka + 4 * l)
                    normalise(R[0], lambda t: xs(X, b, t * P, P), a_mv, a_rs).then_inc(yn_ready, 1)
                if l == 0:
                    if j == 9:
                        dve.wait_ge(proj_used, 5 * ka - 4)
                        link(dve.tensor_scalar(R[1], R[0], cols0[:, 5:6], cols0[:, 7:8], ALU.mult, ALU.add))
                        dve.tensor_scalar(R[0], R[0], cols0[:, 6:7], cols0[:, 8:9], ALU.mult, ALU.add).then_inc(qk_ready, 1)
                    if j in (11, 12):
                        q = j - 11
                        dve.wait_ge(relu_ready, 2 * ka - 1 + q)
                        dve.tensor_tensor(R[6 + q], R[6 + q], R[6 + q], ALU.mult).then_inc(sq_ready, 1)
                    if j in (13, 14):
                        q = j - 13
                        dve.wait_ge(av_ready, 2 * ka - 1 + q)
                        g = tiles(region[:, 2 * NT:4 * NT], NT)[:, :, q * SEQ:(q + 1) * SEQ]
                        dve.tensor_tensor(g, tiles(S[1 - q][:, :], SEQ), g, ALU.mult).then_inc(og_ready, 1)
                    if j == 15:
                        dve.wait_ge(ao_ready, ka)
                        dve.tensor_tensor(xs(X, b), xs(X, b), S[1][:, :], ALU.add).then_inc(x_done, 1)
                        assert link.n == LINKS_A[0], link.n
                else:
                    if j in (9, 10):
                        q = j - 9
                        dve.wait_ge(qkv_ready, 2 * ka - 1 + q)
                        dve.tensor_scalar(tiles(R[2][:, q * SEQ:(q + 1) * SEQ]), tiles(S[q][:, :], 2 * P)[:, :, 0:P], 0.0, None,
                                          ALU.min).then_inc(min_ready, 1)
                    if j == 12:
                        dve.wait_ge(exp_ready, ka)
                        for q in range(2):
                            last = dve.scalar_tensor_tensor(tiles(R[0][:, q * SEQ:(q + 1) * SEQ]), tiles(S[q][:, :], 2 * P)[:, :, 0:P],
                                                            0.0, tiles(R[2][:, q * SEQ:(q + 1) * SEQ]), ALU.max, ALU.add)
                        last.then_inc(phi_ready, 1)
                    if j == 15:
                        dve.wait_ge(kcum_ready, ka)
                        dve.tensor_tensor(tiles(kden[:, :], 64), tiles(S[0][:, 0:TB * 64], 64), tiles(R[0])[:, :, 0:64], ALU.mult).then_inc(den_read, 1)
                        dve.wait_ge(den_read, ka)
                        link(dve.tensor_reduce(den[:, :], kden[:, :].rearrange("p (a f) -> p a f", f=F), AX.X, ALU.add))
                        link(dve.tensor_scalar(den[:, :], den[:, :], 1e-6, None, ALU.add))
                        link(dve.reciprocal(rden[:, :], den[:, :]))
                    if j in (16, 17, 18, 19):
                        t = j - 16
                        dve.wait_ge(cum_ready, 4 * ka - 3 + t)
                        qq = R[0][:, t * P:t * P + 64].rearrange("p (h f) -> p h f", f=F)
                        dve.tensor_tensor(R[2].rearrange("p (h f g) -> p h f g", f=F, g=G),
                                          S[(t + 1) % 2][:, :].rearrange("p (h f g) -> p h f g", f=F, g=G),
                                          qq.unsqueeze(3).to_broadcast([P, HEADS, F, G]), ALU.mult).then_inc(cum_used, 1)
                        dve.wait_ge(cum_used, 4 * ka - 3 + t)
                        link(dve.tensor_reduce(xT[:, t * P:(t + 1) * P].rearrange("p (h g) -> p h g", g=G),
                                               R[2].rearrange("p (h f g) -> p h g f", f=F, g=G), AX.X, ALU.add))
                    if j == 19:
                        o = xT[:, :].rearrange("p (a g) -> p a g", g=G)
                        dve.tensor_tensor(o, o, over(rden[:, :], G), ALU.mult).then_inc(att_ready, 1)
                    if j == 23:
                        dve.wait_ge(ao_ready, NB + ka)
                        assert link.n == LINKS_A[1], link.n
                        dve.tensor_tensor(xs(X, b), xs(X, b), S[0][:, :], ALU.add).then_inc(x_done, 1)

            def sides(s, b, j, state):
                sa, ba = side_after(s, b)
                if sa >= 0:
                    if sa in (0, 2) and j == 0:
                        base = ba * LINKS_A[0] if sa == 0 else NB * LINKS_A[0] + ba * LINKS_A[1]
                        state["alink"] = Links(dve, a_link, base)
                    after_stage(sa, ba, j, state.get("alink"))
                sb_, bb = side_before(s, b)
                if 0 <= sb_ < 3:
                    k = NB * (sb_ + 1) + bb + 1
                    if j == 0:
                        after_apart(dve, spare[:, 0:1], x_done, k - NB)
                    before(layer[sb_ + 1], j, k, bb, state)
                if sa in (0, 2):
                    att_after(sa // 2, sa, ba, j, ba + 1, state["alink"])
                for blk, js in first_prep(s, b, j):
                    if js[0] == 0 and blk == 1:
                        dve.wait_ge(x1_loaded, 16)
                    if js[0] == 0 and blk == 2:
                        dve.wait_ge(x_rest_loaded, 16 * (NB - 2))
                    for j_ in js:
                        if j_ < TAIL:
                            before(0, j_, blk + 1, blk, state)
                if s == 0 and isinstance(b, int) and b == 0 and j == BIAS_AT + 1:
                    dve.wait_ge(bias_hi, 1)
                    dve.scalar_tensor_tensor(brows[:, :], brows[:, :].bitcast(F32), row1[:, 0:1], region[0:2, 5 * NT:5 * NT + BIAS],
                                             ALU.mult, ALU.add).then_inc(bias_split, 1)

            dve.wait_ge(x_loaded, 16)
            dve.wait_ge(consts, 6)
            state = {}
            for j in range(TAIL):
                before(0, j, 1, 0, state)
            done = [len(pieces0)]

            def to_lo(n, j, rows):
                dve.wait_ge(hi_done, n + 1)
                dve.tensor_tensor(in_ring(hL, j, rows), in_ring(hid, j, rows), in_ring(hH, j, rows).bitcast(F32),
                                  ALU.subtract).then_inc(lo_done, 1)

            def body(s, b):
                ex = experts[layer[s]]
                n = step_of(s, b)
                state = {}
                for j in range(steps[s]):
                    rows = ex.rows[j % ex.chunks]
                    dve.wait_ge(silu_done, n + j + 1)
                    h = in_ring(hid, j, rows)
                    dve.tensor_tensor(h, UG[j % 2][0:rows, 0:NT], h, ALU.mult).then_inc(hid_done, 1)
                    first = (s == 0 and isinstance(b, int) and b == 0 and j < RING) or True
                    if first:
                        sides(s, b, j, state)
                    to_split(to_lo, s, b, j)
                    if splits_at(s, b, j):
                        split_lo_piece(done[0])
                        done[0] += 1
                    if not first:
                        sides(s, b, j, state)

            each_body(dve, body)
            for j in range(SPLIT_LAG):
                to_split(to_lo, 4, 0, j)
            sides(4, 0, LAG, {})

        @block.tensor
        def _(pe):
            def before(l, j, k):
                if j == 4:
                    pe.wait_ge(z_ready, k)
                    after(pe, wT_used, k - 1)
                    for t in range(TB):
                        last = pe.transpose(S[2][:, t * P:(t + 1) * P], Z[:, t * P:(t + 1) * P], ident[:, :])
                    last.then_inc(zT_ready, 1)
                if j == 6:
                    pe.wait_ge(xh_ready, k)
                    for t in range(TB):
                        last = pe.matmul(S[2][:, t * E:(t + 1) * E], zT[:, t * P:(t + 1) * P], wr[:, l * E:(l + 1) * E],
                                         start=True, stop=True)
                    last.then_inc(score_ready, 1)
                if j == 14:
                    pe.wait_ge(w_ready, k)
                    for t in range(TB):
                        last = pe.transpose(S[2][0:E, t * P:(t + 1) * P], wt[:, t * E:(t + 1) * E], ident[:, :])
                    last.then_inc(wT_ready, 1)

            def after_stage(s, b, j):
                if j == LAG:
                    m = NB * s + b
                    pe.wait_ge(accT, m + 1)
                    after(pe, x_done, m)
                    for t in range(TB):
                        last = pe.transpose(S[0][:, t * P:(t + 1) * P], R[3][:, t * P:(t + 1) * P], ident[:, :])
                    last.then_inc(acc_tok, 1)

            def att_after(l, j, ka):
                if j == 7:
                    pe.wait_ge(yn_ready, ka + 4 * l)
                    for t in range(TB):
                        last = pe.transpose(S[1][:, t * P:(t + 1) * P], R[0][:, t * P:(t + 1) * P], ident[:, :])
                    last.then_inc(ynT_ready, 1)
                if l == 0:
                    if j == 8:
                        pe.wait_ge(xT_ready, ka)
                        pe.matmul(S[0][:, :], w_qk[:, :], xT[:, :], start=True, stop=True).then_inc(proj_ready, 1)
                    if j in (8, 9):
                        c = j - 8
                        if c:
                            pe.wait_ge(proj_used, 5 * ka - 4)
                        pe.matmul(S[1 - c][:, :], w_hid[:, HID + c * P:HID + (c + 1) * P], xT[:, :], start=True, stop=True).then_inc(proj_ready, 1)
                    if j in (9, 10):
                        q = j - 9
                        pe.wait_ge(proj_used, 5 * ka - 3 + q)
                        for t in range(2):
                            o = S[1 - q][:, t * HID:(t + 1) * HID]
                            pe.matmul(o, xT[:, (2 * q + t) * P:(2 * q + t + 1) * P], w_hid[:, 0:HID], start=True, stop=False)
                            last = pe.matmul(o, onesR[:, :], bias_v, start=False, stop=True)
                        last.then_inc(proj_ready, 1)
                    if j in (10, 11):
                        q = j - 10
                        pe.wait_ge(proj_used, 5 * ka - 1 + q)
                        pe.wait_ge(qk_ready, ka)
                        for t in range(2):
                            last = pe.matmul(S[1 - q][:, t * SEQ:(t + 1) * SEQ], R[0][:, q * SEQ + t * P:q * SEQ + (t + 1) * P],
                                             R[1][:, q * SEQ:(q + 1) * SEQ], start=True, stop=True)
                        last.then_inc(sim_ready, 1)
                    if j in (12, 13):
                        q = j - 12
                        pe.wait_ge(sq_ready, 2 * ka - 1 + q)
                        for c in range(2):
                            for t in range(2):
                                last = pe.matmul(S[1 - q][:, c * SEQ:(c + 1) * SEQ], R[4 + q][:, t * HID + c * P:t * HID + (c + 1) * P],
                                                 R[6 + q][:, t * SEQ:(t + 1) * SEQ], start=(t == 0), stop=(t == 1))
                        last.then_inc(av_ready, 1)
                    if j == 15:
                        pe.wait_ge(og_ready, 2 * ka)
                        for t in range(TB):
                            o = S[1][:, t * P:(t + 1) * P]
                            for c in range(2):
                                pe.matmul(o, R[2 + c][:, t * P:(t + 1) * P], w_o0[:, c * P:(c + 1) * P], start=(c == 0), stop=False)
                            last = pe.matmul(o, onesR[:, :], bias_o0, start=False, stop=True)
                        last.then_inc(ao_ready, 1)
                else:
                    if j in (8, 9):
                        q = j - 8
                        pe.wait_ge(xT_ready, NB + ka)
                        for t in range(2):
                            o = S[q][:, t * 2 * P:(t + 1) * 2 * P]
                            pe.matmul(o, xT[:, (2 * q + t) * P:(2 * q + t + 1) * P], w_qkv[:, :], start=True, stop=False)
                            last = pe.matmul(o, onesR[:, :], bias_qkv, start=False, stop=True)
                        last.then_inc(qkv_ready, 1)
                    if j == 14:
                        pe.wait_ge(phi_ready, ka)
                        for t in range(TB):
                            o = S[0][:, t * 64:(t + 1) * 64]
                            last = pe.matmul(o, tri[:, :], R[0][:, t * P + 64:(t + 1) * P], start=True, stop=(t % 2 == 0))
                            if t % 2:
                                last = pe.matmul(o, ones[:, :], R[0][:, (t - 1) * P + 64:t * P], start=False, stop=True)
                        last.then_inc(kcum_ready, 1)
                    if j in (15, 16, 17, 18):
                        t = j - 15
                        pe.wait_ge(kv_ready, 4 * ka - 3 + t)
                        if t == 0:
                            pe.wait_ge(v_ready, 2 * ka)
                        if t == 1:
                            pe.wait_ge(den_read, ka)
                        if t >= 2:
                            pe.wait_ge(cum_used, 4 * ka - 5 + t)
                        o = S[(t + 1) % 2][:, :]
                        last = pe.matmul(o, tri[:, :], R[3 + t], start=True, stop=(t % 2 == 0))
                        if t % 2:
                            last = pe.matmul(o, ones[:, :], R[2 + t], start=False, stop=True)
                        last.then_inc(cum_ready, 1)
                    if j == 21:
                        pe.wait_ge(att_ready, ka)
                        for t in range(TB):
                            last = pe.transpose(S[1][:, t * P:(t + 1) * P], xT[:, t * P:(t + 1) * P], ident[:, :])
                        last.then_inc(attT_ready, 1)
                    if j == 22:
                        pe.wait_ge(attT_used, ka)
                        for t in range(TB):
                            o = S[0][:, t * P:(t + 1) * P]
                            pe.matmul(o, R[1][:, t * P:(t + 1) * P], w_o1[:, :], start=True, stop=False)
                            last = pe.matmul(o, onesR[:, :], bias_o1, start=False, stop=True)
                        last.then_inc(ao_ready, 1)

            def sides(s, b, j):
                sa, ba = side_after(s, b)
                if sa >= 0:
                    after_stage(sa, ba, j)
                if sa in (0, 2):
                    att_after(sa // 2, j, ba + 1)
                sb_, bb = side_before(s, b)
                if 0 <= sb_ < 3:
                    before(layer[sb_ + 1], j, NB * (sb_ + 1) + bb + 1)
                for blk, js in first_prep(s, b, j):
                    for j_ in js:
                        before(0, j_, blk + 1)

            pe.wait_ge(consts, 6)
            pe.wait_ge(norm_loaded, 32)
            for j in range(TAIL):
                before(0, j, 1)

            def down(l, n, j):
                ex = experts[l]
                c = j % ex.chunks
                rows, at = ex.rows[c], ex.down_at(j // ex.chunks, c)
                pe.wait_ge(lo_done, n + 1)
                if j == 0:
                    after(pe, accT, block_of[0])
                wh, wl = downH[l][0:rows, at:at + P], downL[l][0:rows, at:at + P]
                hh, hl = in_ring(hH, j, rows), in_ring(hL, j, rows)
                pe.matmul(ACC[:, :], wh, hh, start=(j == 0), stop=False)
                pe.matmul(ACC[:, :], wh, hl, start=False, stop=False)
                pe.matmul(ACC[:, :], wl, hh, start=False, stop=(j == ex.steps - 1)).then_inc(down_done, 1)

            block_of = [0]

            def body(s, b):
                l = layer[s]
                ex = experts[l]
                n = step_of(s, b)
                block_of[0] = NB * s + b
                for j in range(steps[s]):
                    e, c = j // ex.chunks, j % ex.chunks
                    rows, at = ex.rows[c], ex.up_at(e, c)
                    if j == 0:
                        pe.wait_ge(xl_ready, NB * s + b + 1)
                    if s == 0 and isinstance(b, int) and b == 0 and c == 0:
                        pe.wait_ge(split_lo0, up_piece[e] + 1)
                    if s == 2 and isinstance(b, int) and b == 0 and j == 0:
                        pe.wait_ge(split_lo1, len(pieces1))
                    after(pe, hid_done, n + j - 1)
                    for half in range(2):
                        cols = slice(at + half * rows, at + (half + 1) * rows)
                        o = UG[j % 2][0:rows, half * NT:(half + 1) * NT]
                        pe.matmul(o, upH[l][:, cols], xs(xH, b), start=True, stop=False)
                        pe.matmul(o, upH[l][:, cols], xs(xL, b), start=False, stop=False)
                        last = pe.matmul(o, upL[l][:, cols], xs(xH, b), start=False, stop=True)
                    last.then_inc(up_done, 1)
                    if j >= LAG:
                        if s == 0 and isinstance(b, int) and b == 0:
                            e_, c_ = (j - LAG) // ex.chunks, (j - LAG) % ex.chunks
                            pe.wait_ge(split_lo0, down_piece[c_, e_ // 4] + 1)
                            if j == steps[0] - 1:
                                pe.wait_ge(bias_split, 1)
                        down(l, n + j - LAG, j - LAG)
                    elif prev_layer(s, b) is not None:
                        down(prev_layer(s, b), n + j - LAG, steps[side_after(s, b)[0]] + j - LAG)
                    sides(s, b, j)

            each_body(pe, body)
            for j in range(LAG):
                down(1, first_step[4] + j - LAG, steps[3] + j - LAG)
            sides(4, 0, LAG)


_OUTS = [((8, 256, 128), "float32")]


def kernel(**inputs):
    import numpy as np
    import concourse.bacc as bacc
    from concourse.bass_utils import run_bass_kernel_spmd

    g = {k: np.asarray(v) for k, v in inputs.items()}

    def up(w, hidden):
        e = w.shape[0]
        parts = []
        for c in range(0, hidden, P):
            n = min(P, hidden - c)
            parts += [w[:, c:c + n, :], w[:, hidden + c:hidden + c + n, :]]
        return np.concatenate(parts, axis=1).transpose(2, 0, 1).reshape(P, e * 2 * hidden)

    def down(w, first, last, rows):
        n = (last - first) // rows
        return w[:, :, first:last].reshape(w.shape[0], P, n, rows).transpose(3, 2, 0, 1).reshape(rows, n * w.shape[0] * P)

    def cols(*vectors):
        return np.stack(vectors, axis=1)

    bh, osw, osb = g["L0_attn_b_hidden"], g["L0_attn_os_weight"], g["L0_attn_os_bias"]
    w1d = g["L1_ffn_w_down"]
    arrays = {
        "x": g["L0_attn_x"].reshape(-1, P),
        "up0": up(g["L0_ffn_w_up"], 256),
        "down0": down(g["L0_ffn_w_down"], 0, 256, P),
        "up1": up(g["L1_ffn_w_up"], 352),
        "down1a": down(w1d, 0, 256, P),
        "down1b": down(w1d, 256, 352, 96),
        "router": np.concatenate([g["L0_ffn_w_router"].T, g["L1_ffn_w_router"].T], axis=1),
        "norm": cols(g["L0_ffn_norm_scale"], g["L1_ffn_norm_scale"]),
        "att0_w": g["L0_attn_W_hidden"],
        "att0_qk": g["L0_attn_W_qk"],
        "att0_out": g["L0_attn_W_out"].reshape(2, P, P).transpose(1, 0, 2).reshape(P, 2 * P),
        "att0_cols": cols(g["L0_attn_ln_scale"], g["L0_attn_ln_bias"], g["L0_attn_b_qk"], bh[HID:HID + P], bh[HID + P:],
                          osw[0], osw[1], osb[0], osb[1]),
        "att1_w": np.concatenate([g["L1_attn_wq"], g["L1_attn_wk"], g["L1_attn_wv"]], axis=1),
        "att1_out": g["L1_attn_wo"],
        "bias_rows": np.stack([np.concatenate([bh[:HID], g["L0_attn_b_out"], g["L1_attn_bq"], g["L1_attn_bk"],
                                               g["L1_attn_bv"], g["L1_attn_bo"]])] * 2),
    }
    nc = bacc.Bacc("TRN2", target_bir_lowering=False, num_devices=1)
    feed, args = {}, []
    for name, a in arrays.items():
        a = np.ascontiguousarray(a)
        feed[f"in_{name}"] = a
        args.append(nc.dram_tensor(f"in_{name}", a.shape, mybir.dt.from_np(a.dtype), kind="ExternalInput").ap())
    args.append(nc.dram_tensor("out", [2048, P], F32, kind="ExternalOutput").ap())
    macaron(nc, *args)
    r = run_bass_kernel_spmd(nc, [feed], core_ids=[0])
    return r.results[0]["out"].reshape(8, 256, 128)
```

```python
import concourse.bass as bass
from concourse import mybir
from contextlib import ExitStack

F32 = mybir.dt.float32
F32R = mybir.dt.float32r
ALU = mybir.AluOpType
ACT = mybir.ActivationFunctionType
AX = mybir.AxisListType

P = 128
NT = 512
TB = NT // P
E = 8
SEQ = 256
HID = 256
HEADS, F, G = 16, 4, 8
LAG = 4
RING = 4
WTILES = 3
SPLIT_LAG = 2
BIAS = 2 * HID + 2 * P
HUGE = 3.0e38


class Experts:

    def __init__(self, hidden, groups, hid_groups):
        assert E * hidden % P == 0
        self.steps = E * hidden // P
        self.slot = [i for g in groups for i in range(g)]
        self.hid_slot = [i for g in hid_groups for i in range(g)]
        assert len(self.slot) == len(self.hid_slot) == self.steps
        assert max(groups) <= RING and max(hid_groups) <= RING + 1
        self.tile_of, self.tile_last, self.tile_parts = [], [], []
        for c in range(self.steps):
            a, z = c * P, (c + 1) * P
            parts = [(max(a, e * hidden) - a, min(z, (e + 1) * hidden) - a, e) for e in range(E)
                     if a < (e + 1) * hidden and z > e * hidden]
            if not self.tile_parts or self.tile_parts[-1] != parts:
                self.tile_parts.append(parts)
                self.tile_last.append(c)
            self.tile_last[-1] = c
            self.tile_of.append(len(self.tile_parts) - 1)

    def loads(self, slot, upto=None):
        tiles = range(len(self.tile_parts) if upto is None else upto + 1)
        return sum(len(self.tile_parts[t]) for t in tiles if t % WTILES == slot)


def after(eng, sem, count):
    if not (isinstance(count, int) and count <= 0):
        eng.wait_ge(sem, count)


def after_apart(eng, cell, sem, count):
    eng.wait_ge(sem, count)
    if not isinstance(count, int):
        eng.memset(cell, 0.0)


class Links:

    def __init__(self, eng, sem, base):
        self.eng, self.sem, self.base, self.n = eng, sem, base, 0

    def __call__(self, ins, apart=None):
        self.n += 1
        ins.then_inc(self.sem, 1)
        if apart is None:
            self.eng.wait_ge(self.sem, self.base + self.n)
        else:
            after_apart(self.eng, apart, self.sem, self.base + self.n)


def macaron(nc, x, up0, down0, up1, down1, router, norm, att0_w, att0_qk, att0_out, att0_cols,
            att1_w, att1_out, bias_rows, out):
    experts = [Experts(256, [4] * 4, [4] * 4), Experts(352, [4, 4, 3, 4, 4, 3], [5, 5, 4, 4, 4])]
    layer = [0, 0, 1, 1]
    NB = x.shape[0] // NT
    steps = [experts[l].steps for l in layer]
    first_step = [NB * sum(steps[:s]) for s in range(5)]
    ctx = ExitStack()
    with ctx:
        def sb(name, cols, dt=F32, rows=P):
            return ctx.enter_context(nc.sbuf_tensor(name, [rows, cols], dt))

        def sem(name):
            return ctx.enter_context(nc.semaphore(name))

        upH = [sb(f"up{l}_hi", 2 * P * experts[l].steps, F32R) for l in range(2)]
        upL = [sb(f"up{l}_lo", 2 * P * experts[l].steps, F32R) for l in range(2)]
        downH = [sb(f"down{l}_hi", P * experts[l].steps, F32R) for l in range(2)]
        downL = [sb(f"down{l}_lo", P * experts[l].steps, F32R) for l in range(2)]
        X = sb("x_res", NB * NT)
        xH = sb("xn_hi", NB * NT, F32R)
        xL = sb("xn_lo", NB * NT, F32R)
        hid = sb("hidden", RING * NT)
        hH = sb("hidden_hi", RING * NT, F32R)
        hL = sb("hidden_lo", RING * NT, F32R)
        wtok = sb("token_weights", WTILES * NT)
        region = sb("attention", 8 * NT)
        R = [region[:, i * NT:(i + 1) * NT] for i in range(8)]
        xT = sb("attn_xT", NT)
        spare = sb("spare", 2)
        a_st = sb("a_stats", TB * 6)
        a_mv = sb("a_meanvar", TB * 2)
        a_ve = sb("a_var", TB)
        a_rs = sb("a_rstd", TB)
        kden = sb("k_den", TB * 64)
        den = sb("den", TB * HEADS)
        rden = sb("rden", TB * HEADS)
        Z = sb("rms_out", NT)
        zT = Z
        stage2 = [sb(f"weight_stage{i}", NT) for i in range(2)]
        b_st = sb("b_stats", TB * 6)
        b_mv = sb("b_meanvar", TB * 2)
        b_ve = sb("b_var", 2 * TB)
        b_rs = sb("b_rstd", 2 * TB)
        b_mul = sb("b_skip_mul", TB)
        b_add = sb("b_skip_add", TB)
        m1 = sb("top1", TB)
        m2 = sb("top2", TB)
        pm = sb("pick", TB)
        e1 = sb("is_max", TB * E)
        oh1 = sb("first", TB * E)
        oh2 = sb("second", TB * E)
        rest = sb("rest", TB * E)
        th = sb("tanh", TB * E)
        thn = sb("one_minus", TB * E)
        w1 = sb("w_first", TB)
        w2 = sb("w_second", TB)
        wt = sb("w_tok", TB * E)
        wtT = sb("w_tokT", P, rows=TB * E)
        ident = sb("ident", P)
        ones = sb("ones", P)
        tri = sb("tri", P)
        mhalf = sb("minus_half", 2 * TB)
        row1 = sb("minus_row1", 1, rows=2)
        onesR = sb("ones_r", P, F32R, rows=2)
        brows = sb("bias_rows", BIAS, F32R, rows=2)
        bias_v, bias_o0, bias_qkv, bias_o1 = (brows[:, a:z] for a, z in ((0, HID), (HID, HID + P), (HID + P, 2 * HID + P), (2 * HID + P, BIAS)))
        prio = sb("priority", TB * E)
        wr = sb("router", 2 * E)
        wn = sb("norm", 2)
        w_hid = sb("a0_hidden", 2 * HID)
        w_qk = sb("a0_qk", P)
        w_o0 = sb("a0_out", 2 * P)
        cols0 = sb("a0_cols", 9)
        w_qkv = sb("a1_qkv", 2 * P)
        w_o1 = sb("a1_out", P)

        UG = [ctx.enter_context(nc.psum_tensor(f"up_gate{i}", [P, 2 * NT], F32)) for i in range(2)]
        ACC = ctx.enter_context(nc.psum_tensor("acc", [P, NT], F32))
        S = [ctx.enter_context(nc.psum_tensor(f"side{i}", [P, NT], F32)) for i in range(3)]
        WD = nc.dram_tensor("token_weights_dram", [NB * TB * E, P], F32, kind="Internal").ap()
        WD_row = WD.rearrange("(b t e) p -> b e t p", b=NB, t=TB)

        x_loaded = sem("x_loaded")
        small_loaded = sem("small_loaded")
        norm_loaded = sem("norm_loaded")
        x_rest_loaded = sem("x_rest_loaded")
        x1_loaded = sem("x1_loaded")
        stage_loaded = [sem(f"stage_loaded{i}") for i in range(6)]
        wtok_loaded = [sem(f"wtok_loaded{i}") for i in range(WTILES)]
        bias_hi, bias_split = sem("bias_hi"), sem("bias_split")
        wd_stored = sem("wd_stored")
        out_stored = sem("out_stored")
        consts = sem("consts")
        const_base = sem("const_base")
        split_hi = sem("split_hi")
        split_lo0, split_lo1 = sem("split_lo0"), sem("split_lo1")
        up_done = sem("up_done")
        silu_done = sem("silu_done")
        hid_done = sem("hid_done")
        scaled = sem("scaled")
        hi_done = sem("hi_done")
        lo_done = sem("lo_done")
        down_done = sem("down_done")
        accT = sem("acc_evacuated")
        acc_tok = sem("acc_token_major")
        x_done = sem("x_done")
        ln1_var, ln1_rstd = sem("ln1_var"), sem("ln1_rstd")
        yn_ready, ynT_ready, xT_ready = sem("yn_ready"), sem("ynT_ready"), sem("xT_ready")
        proj_ready, proj_used = sem("proj_ready"), sem("proj_used")
        qk_ready, sim_ready, relu_ready, sq_ready = sem("qk_ready"), sem("sim_ready"), sem("relu_ready"), sem("sq_ready")
        av_ready, og_ready, ao_ready = sem("av_ready"), sem("og_ready"), sem("ao_ready")
        qkv_ready, min_ready, v_ready, exp_ready = sem("qkv_ready"), sem("min_ready"), sem("v_ready"), sem("exp_ready")
        phi_ready, kv_ready, kcum_ready, den_read = sem("phi_ready"), sem("kv_ready"), sem("kcum_ready"), sem("den_read")
        cum_ready, cum_used = sem("cum_ready"), sem("cum_used")
        att_ready, attT_ready, attT_used = sem("att_ready"), sem("attT_ready"), sem("attT_used")
        a_link = sem("a_link")
        b_var, b_rstd, skip_ready = sem("b_var"), sem("b_rstd"), sem("skip_ready")
        z_ready, zT_ready, zT_used, xh_ready = sem("z_ready"), sem("zT_ready"), sem("zT_used"), sem("xh_ready")
        score_ready, d_ready, th_ready = sem("score_ready"), sem("d_ready"), sem("th_ready")
        w_ready, wT_ready, wT_used, xl_ready = sem("w_ready"), sem("wT_ready"), sem("wT_used"), sem("xl_ready")
        b_link = sem("b_link")

        SKIP_AT = 11
        EXP_AT = 11
        BIAS_AT = 12
        BSTEPS = 16
        LINKS_B = [20, 23]
        LINKS_A = [5, 10]

        def in_ring(t, l, j):
            k = experts[l].slot[j]
            return t[:, k * NT:(k + 1) * NT]

        def hid_ring(l, j):
            k = experts[l].hid_slot[j]
            return hid[:, k * NT:(k + 1) * NT] if k < RING else stage2[0][:, :]

        def reuse(slots, before, j):
            for d in range(1, j + len(before) + 1):
                if (slots[j - d] if d <= j else before[j - d]) == slots[j]:
                    return d
            return None

        def reuse_hid(l, lp, j):
            return reuse(experts[l].hid_slot, experts[lp].hid_slot if lp is not None else [], j)

        def reuse_split(l, lp, j):
            return reuse(experts[l].slot, experts[lp].slot if lp is not None else [], j)

        def wtile(t):
            return wtok[:, (t % WTILES) * NT:(t % WTILES + 1) * NT]

        def wtok_count(s, b, t):
            k = t % WTILES
            return 16 * (NB * sum(experts[l].loads(k) for l in layer[:s]) + experts[layer[s]].loads(k, t)) \
                + b * (16 * experts[layer[s]].loads(k))

        def pieces(src, hi, lo):
            n = src.shape[1]
            return [tuple(a[:, c:min(c + NT, n)] for a in (src, hi, lo)) for c in range(0, n, NT)]

        up_piece = [0, 1, 2, 4, 5, 7, 8, 10]
        down_piece = [3, 6, 9, 11]
        pieces0 = [None] * 12
        for at, found in ((up_piece, pieces(up0, upH[0], upL[0])), (down_piece, pieces(down0, downH[0], downL[0]))):
            assert len(at) == len(found)
            for n, piece in zip(at, found):
                pieces0[n] = piece
        pieces1 = pieces(up1, upH[1], upL[1]) + pieces(down1, downH[1], downL[1])
        split_all = pieces0 + pieces1

        HI_BEFORE, HI_STEP = 5, 0
        LO_BEFORE, LO_STEP = 7, 2
        LO_FIRST = 6
        LOAD_BEFORE = 8

        def piece_at(before, first, s, b, j):
            n = before + j - first
            return n if s == 0 and isinstance(b, int) and b == 0 and j >= first and n < len(pieces0) else None

        split_steps = {(0, 1): (0, 2, 12, 14), (1, 0): (0, 2, 12, 14), (1, 1): (2, 4, 5, 6, 9, 11, 13, 14, 15)}
        assert sum(map(len, split_steps.values())) == len(pieces1)

        def splits_at(s, b, j):
            return isinstance(b, int) and j in split_steps.get((s, b), ())

        def staging(n):
            n0 = len(pieces0)
            if n < n0:
                return R[n % 4], stage_loaded[n % 4], 16 * (n // 4 + 1), split_lo0, n - 3
            return stage2[n % 2], stage_loaded[4 + n % 2], 16 * ((n - n0) // 2 + 1), split_lo1, n - n0 - 1

        def each_body(eng, body):
            for s in range(4):
                body(s, 0)
                body(s, 1)
                with eng.Fori(2, NB) as b:
                    body(s, b)

        def side_after(s, b):
            return (s, b - 1) if not (isinstance(b, int) and b == 0) else (s - 1, NB - 1)

        def side_before(s, b):
            return (s, b - 2) if not (isinstance(b, int) and b < 2) else (s - 1, b + NB - 2)

        TWO_IN_ONE = ((0, 1), (2, 3), (4, 5), (6, 7), (8, 9), (10, 11), (12, 13), (14, 15))
        TAIL = 13

        def first_prep(s, b, j):
            if s or not isinstance(b, int) or b > 1:
                return []
            if b == 1:
                return [(3, (j,))]
            n = len(TWO_IN_ONE)
            tail = [(0, tuple(range(TAIL, BSTEPS)))] if j == 0 else []
            return tail + [(1 + j // n, TWO_IN_ONE[j % n])]

        def step_of(s, b):
            return first_step[s] + (b * steps[s] if s < 4 else 0)

        def prev_layer(s, b):
            return layer[side_after(s, b)[0]] if side_after(s, b)[0] >= 0 else None

        def to_split(split, s, b, j):
            if j >= SPLIT_LAG:
                split(step_of(s, b) + j - SPLIT_LAG, layer[s], prev_layer(s, b), j - SPLIT_LAG)
            elif prev_layer(s, b) is not None:
                lp = prev_layer(s, b)
                split(step_of(s, b) + j - SPLIT_LAG, lp, lp, experts[lp].steps + j - SPLIT_LAG)

        def xs(t, b, at=0, n=NT):
            if isinstance(b, int):
                return t[:, b * NT + at:b * NT + at + n]
            return t[:, bass.ds(b * NT + at, n)]

        def tiles(ap, cols=P):
            return ap.rearrange("p (t c) -> p t c", c=cols)

        def over(ap, n):
            return ap.unsqueeze(2).to_broadcast([ap.shape[0], ap.shape[1], n])

        block = ctx.enter_context(nc.Block())

        @block.sync
        def _(sp):
            def load_x(b, loaded):
                sp.dma_start(tiles(xs(X, b)), x[b * NT:(b + 1) * NT, :].rearrange("(t p) d -> p t d", p=P)).then_inc(loaded, 16)

            def load_piece(n):
                src = split_all[n][0]
                buf, loaded, _, split_lo, gone = staging(n)
                after(sp, split_lo, gone)
                sp.dma_start(buf[:, 0:src.shape[1]], src).then_inc(loaded, 16)

            load_x(0, x_loaded)
            sp.dma_start(wn[:, :], norm).then_inc(norm_loaded, 16)
            sp.dma_start(wr[:, :], router).then_inc(norm_loaded, 16)
            for n in range(LOAD_BEFORE):
                load_piece(n)
                if n == 1:
                    load_x(1, x1_loaded)
                if n == 5:
                    for b in range(2, NB):
                        load_x(b, x_rest_loaded)

            def load_small():
                small = ((w_hid, att0_w), (w_qk, att0_qk), (w_o0, att0_out), (cols0, att0_cols), (w_qkv, att1_w), (w_o1, att1_out))
                for dst, src in small:
                    sp.dma_start(dst[:, :], src).then_inc(small_loaded, 16)
                sp.dma_start(region[0:2, 5 * NT:5 * NT + BIAS], bias_rows).then_inc(small_loaded, 16)

            def store_out(b):
                after(sp, x_done, 3 * NB + b + 1)
                rows = out[b * NT:(b + 1) * NT, :] if isinstance(b, int) else out[bass.ds(b * NT, NT), :]
                sp.dma_start(rows.rearrange("(t p) d -> p t d", p=P), tiles(xs(X, b))).then_inc(out_stored, 16)

            to_load = [LOAD_BEFORE]

            def body(s, b):
                ex = experts[layer[s]]
                m = NB * s + b
                after(sp, wd_stored, 16 * (m + 1))
                for t, parts in enumerate(ex.tile_parts):
                    if t >= WTILES:
                        after(sp, scaled, step_of(s, b) + ex.tile_last[t - WTILES] + 1)
                    elif prev_layer(s, b) is not None:
                        old = experts[prev_layer(s, b)]
                        told = [u for u in range(len(old.tile_last)) if u % WTILES == t][-1]
                        after(sp, scaled, step_of(s, b) - old.steps + old.tile_last[told] + 1)
                    for first, last, e in parts:
                        row = WD_row[b:b + 1, e] if isinstance(b, int) else WD_row[bass.ds(b, 1), e]
                        sp.dma_start(tiles(wtile(t)[first:last, :]), row.to_broadcast([last - first, TB, P])).then_inc(wtok_loaded[t % WTILES], 16)
                    if s == 0 and isinstance(b, int) and b == 0:
                        if t == 4:
                            load_small()
                        for _ in {1: range(3), 3: range(1), 5: range(2)}.get(t, ()):
                            load_piece(to_load[0])
                            to_load[0] += 1
                    if s < 2 and isinstance(b, int):
                        for j in range(ex.steps):
                            if ex.tile_of[j] == t and splits_at(s, b, j) and to_load[0] < len(split_all):
                                load_piece(to_load[0])
                                to_load[0] += 1
                if s == 3 and not (isinstance(b, int) and b == 0):
                    store_out(b - 1)

            each_body(sp, body)
            store_out(NB - 1)
            sp.wait_ge(out_stored, 16 * NB)

        @block.gpsimd
        def _(pool):
            pool.memset(ident[:, :], 0.0).then_inc(const_base, 1)
            pool.memset(tri[:, :], 1.0).then_inc(const_base, 1)
            pool.memset(ones[:, :], 1.0).then_inc(consts, 1)
            pool.memset(mhalf[:, :], -0.5).then_inc(consts, 1)
            for e in range(E):
                last = pool.memset(tiles(prio[:, :], E)[:, :, e:e + 1], float(E - e))
            last.then_inc(consts, 1)
            pool.memset(row1[:, :], -1.0).then_inc(const_base, 1)
            pool.wait_ge(const_base, 3)
            pool.affine_select(out=ident[:, :], in_=ident[:, :], compare_op=ALU.not_equal, fill=1.0, base=0,
                               pattern=[[-1, P]], channel_multiplier=1).then_inc(consts, 1)
            pool.affine_select(out=row1[:, :], in_=row1[:, :], compare_op=ALU.is_gt, fill=0.0, base=0,
                               pattern=[[0, 1]], channel_multiplier=1).then_inc(consts, 1)
            pool.affine_select(out=tri[:, :], in_=tri[:, :], compare_op=ALU.is_ge, fill=0.0, base=0,
                               pattern=[[1, P]], channel_multiplier=-1).then_inc(consts, 1)
            pool.wait_ge(consts, 6)

            def before(l, j, k, b):
                if j == 1:
                    pool.wait_ge(b_var, k)
                    pool.tensor_tensor(b_rs[:, :], b_ve[:, :], mhalf[:, :], ALU.pow).then_inc(b_rstd, 1)

            def att_after(l, j, ka):
                if j == 5:
                    pool.wait_ge(ln1_var, ka + 4 * l)
                    pool.tensor_tensor(a_rs[:, :], a_ve[:, :], mhalf[:, 0:TB], ALU.pow).then_inc(ln1_rstd, 1)
                if l == 1 and j in (13, 14, 15, 16):
                    t = j - 13
                    if t == 0:
                        pool.wait_ge(phi_ready, ka)
                    if t % 2 == 0:
                        pool.wait_ge(v_ready, 2 * ka - 1 + t // 2)
                    kk = R[0][:, t * P + 64:(t + 1) * P].rearrange("p (h f) -> p h f", f=F)
                    vv = R[1][:, t * P:(t + 1) * P].rearrange("p (h g) -> p h g", g=G)
                    pool.tensor_tensor(R[3 + t].rearrange("p (h f g) -> p h f g", f=F, g=G),
                                       kk.unsqueeze(3).to_broadcast([P, HEADS, F, G]),
                                       vv.unsqueeze(2).to_broadcast([P, HEADS, F, G]), ALU.mult).then_inc(kv_ready, 1)

            def sides(s, b, j):
                sa, ba = side_after(s, b)
                if sa in (0, 2):
                    att_after(sa // 2, j, ba + 1)
                sb_, bb = side_before(s, b)
                if 0 <= sb_ < 3:
                    before(layer[sb_ + 1], j, NB * (sb_ + 1) + bb + 1, bb)
                for blk, js in first_prep(s, b, j):
                    for j_ in js:
                        before(0, j_, blk + 1, blk)

            def split_lo_piece(n):
                _, hi, lo = pieces0[n]
                pool.wait_ge(split_hi, n + 1)
                pool.tensor_tensor(lo, staging(n)[0], hi.bitcast(F32), ALU.subtract).then_inc(split_lo0, 1)

            for j in range(TAIL):
                before(0, j, 1, 0)
            for n in range(LO_FIRST):
                split_lo_piece(n)

            def body(s, b):
                ex = experts[layer[s]]
                n = step_of(s, b)
                for j in range(steps[s]):
                    t = ex.tile_of[j]
                    first = s == 0 and isinstance(b, int) and b == 0 and j == 0
                    if first:
                        sides(s, b, j)
                        for n_ in range(LO_FIRST, LO_BEFORE):
                            split_lo_piece(n_)
                    if j == 0 or t != ex.tile_of[j - 1]:
                        pool.wait_ge(wtok_loaded[t % WTILES], wtok_count(s, b, t))
                    pool.wait_ge(hid_done, n + j + 1)
                    h = hid_ring(layer[s], j)
                    pool.tensor_tensor(h, h, wtile(t), ALU.mult).then_inc(scaled, 1)
                    if piece_at(LO_BEFORE, LO_STEP, s, b, j) is not None:
                        split_lo_piece(piece_at(LO_BEFORE, LO_STEP, s, b, j))
                    if not first:
                        sides(s, b, j)

            each_body(pool, body)

        @block.scalar
        def _(act):
            def split_hi_piece(n):
                hi = split_all[n][1]
                buf, loaded, value = staging(n)[:3]
                act.wait_ge(loaded, value)
                act.activation(hi, buf[:, 0:hi.shape[1]], ACT.Copy).then_inc(split_hi, 1)

            def before(l, j, k, b):
                if j == 4:
                    act.wait_ge(zT_ready, k)
                    act.activation(zT[:, :], S[2][:, :], ACT.Copy, scale=wn[:, l:l + 1]).then_inc(zT_used, 1)
                    act.activation(xs(xH, b), S[2][:, :], ACT.Copy, scale=wn[:, l:l + 1]).then_inc(xh_ready, 1)
                if j == 10:
                    act.wait_ge(d_ready, k)
                    if l == 0:
                        act.activation(th[:, 0:TB], w1[:, :], ACT.Tanh, scale=0.5).then_inc(th_ready, 1)
                    else:
                        act.activation(th[:, :], rest[:, :], ACT.Tanh, scale=0.5).then_inc(th_ready, 1)
                if j == 15:
                    act.wait_ge(wT_ready, k)
                    after(act, wd_stored, 16 * (k - 1))
                    act.activation(wtT[:, :], S[2][0:TB * E, 0:P], ACT.Copy).then_inc(wT_used, 1)
                    act.wait_ge(wT_used, k)
                    n = TB * E
                    rows = WD[b * n:(b + 1) * n, :] if isinstance(b, int) else WD[bass.ds(b * n, n), :]
                    act.dma_start(rows, wtT[:, :]).then_inc(wd_stored, 16)

            def after_stage(s, b, j):
                if j == LAG - 1:
                    m = NB * s + b
                    act.wait_ge(down_done, step_of(s, b) + steps[s])
                    after(act, x_done, m)
                    act.activation(R[3], ACC[:, :], ACT.Copy).then_inc(accT, 1)

            def att_after(l, j, ka):
                if j == 7:
                    act.wait_ge(ynT_ready, ka + 4 * l)
                    if l == 0:
                        act.activation(xT[:, :], S[1][:, :], ACT.Identity, scale=cols0[:, 0:1], bias=cols0[:, 1:2]).then_inc(xT_ready, 1)
                    else:
                        act.activation(xT[:, :], S[1][:, :], ACT.Copy).then_inc(xT_ready, 1)
                if l == 0:
                    for i in {8: (0, 1), 9: (2, 3), 10: (4,)}.get(j, ()):
                        act.wait_ge(proj_ready, 5 * ka - 4 + i)
                        dst, src, bias = ((R[0], S[0], cols0[:, 2:3]), (R[2], S[1], cols0[:, 3:4]), (R[3], S[0], cols0[:, 4:5]),
                                          (R[4], S[1], 0.0), (R[5], S[0], 0.0))[i]
                        act.activation(dst, src[:, :], ACT.Silu, bias=bias).then_inc(proj_used, 1)
                    if j in (11, 12):
                        q = j - 11
                        act.wait_ge(sim_ready, 2 * ka - 1 + q)
                        act.activation(R[6 + q], S[1 - q][:, :], ACT.Relu, scale=1.0 / SEQ).then_inc(relu_ready, 1)
                else:
                    if j in (10, 13):
                        q = (j - 10) // 3
                        if q == 0:
                            act.wait_ge(min_ready, 2 * ka - 1)
                        else:
                            act.wait_ge(phi_ready, ka)
                        act.activation(tiles(R[1][:, q * SEQ:(q + 1) * SEQ]), tiles(S[q][:, :], 2 * P)[:, :, P:2 * P], ACT.Copy).then_inc(v_ready, 1)
                    if j == EXP_AT:
                        act.wait_ge(min_ready, 2 * ka)
                        act.activation(R[2], R[2], ACT.Exp).then_inc(exp_ready, 1)
                        act.activation(spare[:, 1:2], ones[:, 0:1], ACT.Silu)
                    if j == 20:
                        act.wait_ge(attT_ready, ka)
                        act.activation(R[1], S[1][:, :], ACT.Copy).then_inc(attT_used, 1)

            def sides(s, b, j):
                sa, ba = side_after(s, b)
                if sa >= 0:
                    after_stage(sa, ba, j)
                if sa in (0, 2):
                    att_after(sa // 2, j, ba + 1)
                sb_, bb = side_before(s, b)
                if 0 <= sb_ < 3:
                    before(layer[sb_ + 1], j, NB * (sb_ + 1) + bb + 1, bb)
                for blk, js in first_prep(s, b, j):
                    for j_ in js:
                        before(0, j_, blk + 1, blk)
                if s == 0 and isinstance(b, int) and b == 0 and j == BIAS_AT:
                    act.activation(onesR[:, :], ones[0:2, :], ACT.Copy)
                    act.wait_ge(small_loaded, 16 * 7)
                    act.activation(brows[:, :], region[0:2, 5 * NT:5 * NT + BIAS], ACT.Copy).then_inc(bias_hi, 1)

            act.wait_ge(consts, 6)
            act.activation(th[:, 0:1], ones[:, 0:1], ACT.Silu)
            split_hi_piece(0)
            act.wait_ge(norm_loaded, 32)
            for j in range(TAIL):
                before(0, j, 1, 0)
                for n in {4: (1, 2), 10: range(3, HI_BEFORE)}.get(j, ()):
                    split_hi_piece(n)
            done = [len(pieces0)]

            def to_hi(n, l, lp, j):
                act.wait_ge(scaled, n + 1)
                if reuse_split(l, lp, j):
                    act.wait_ge(down_done, n + 1 - reuse_split(l, lp, j))
                act.activation(in_ring(hH, l, j), hid_ring(l, j), ACT.Copy).then_inc(hi_done, 1)

            def body(s, b):
                ex = experts[layer[s]]
                n = step_of(s, b)
                for j in range(steps[s]):
                    exp_step = j == EXP_AT and side_after(s, b)[0] == 2
                    if exp_step:
                        to_split(to_hi, s, b, j)
                    act.wait_ge(up_done, n + j + 1)
                    back = reuse_hid(layer[s], prev_layer(s, b), j)
                    if back:
                        act.wait_ge(lo_done, n + j + 1 - back)
                    act.activation(hid_ring(layer[s], j), UG[j % 2][:, NT:2 * NT], ACT.Silu).then_inc(silu_done, 1)
                    sides_first = j != 4
                    if sides_first:
                        sides(s, b, j)
                    if not exp_step:
                        to_split(to_hi, s, b, j)
                    if piece_at(HI_BEFORE, HI_STEP, s, b, j) is not None:
                        split_hi_piece(piece_at(HI_BEFORE, HI_STEP, s, b, j))
                    if splits_at(s, b, j):
                        split_hi_piece(done[0])
                        done[0] += 1
                    if not sides_first:
                        sides(s, b, j)

            each_body(act, body)
            for j in range(SPLIT_LAG):
                to_split(to_hi, 4, 0, j)
            sides(4, 0, LAG - 1)

        @block.vector
        def _(dve):
            def split_lo_piece(n):
                _, hi, lo = split_all[n]
                dve.wait_ge(split_hi, n + 1)
                dve.tensor_tensor(lo, staging(n)[0][:, 0:hi.shape[1]], hi.bitcast(F32), ALU.subtract).then_inc(split_lo1, 1)

            def stats(link, src, st, mv, ve, eps2, alone, done, first=0, part=(0, 1)):
                if 0 in part:
                    for t in range(first, TB):
                        last = dve.bn_stats(st[:, 6 * t:6 * t + 6], src(t))
                    link(last, apart=spare[:, 0:1])
                if 1 not in part:
                    return
                for t in range(TB):
                    last = dve.bn_aggr(mv[:, 2 * t:2 * t + 2], st[:, 6 * t:6 * t + 6])
                link(last)
                var = mv[:, 1:2 * TB:2]
                ins = dve.tensor_scalar(ve[:, 0:TB], var, 1e-5, None, ALU.add)
                if eps2 is not None:
                    link(ins)
                    both = ve[:, TB:2 * TB] if alone else ve[:, 0:TB]
                    ins = dve.scalar_tensor_tensor(both, ve[:, 0:TB], eps2, var, ALU.mult, ALU.add)
                ins.then_inc(done, 1)

            def normalise(dst, src, mv, rs):
                for t in range(TB):
                    last = dve.tensor_scalar(dst[:, t * P:(t + 1) * P], src(t), mv[:, 2 * t:2 * t + 1], rs[:, t:t + 1],
                                             ALU.subtract, ALU.mult)
                return last

            def before(l, j, k, b, state):
                if j == 0:
                    base = (k - 1) * LINKS_B[0] if l == 0 else 2 * NB * LINKS_B[0] + (k - 1 - 2 * NB) * LINKS_B[1]
                    state["link"] = Links(dve, b_link, base)
                    for t in range(2):
                        dve.bn_stats(b_st[:, 6 * t:6 * t + 6], xs(X, b, t * P, P))
                if j == 1:
                    stats(state["link"], lambda t: xs(X, b, t * P, P), b_st, b_mv, b_ve, 1e-6, True, b_var, first=2)
                link = state["link"]
                sc = tiles(S[2][:, 0:TB * E], E)
                v = lambda t: tiles(t[:, :], E)
                if j == 3:
                    dve.wait_ge(b_rstd, k)
                    normalise(Z, lambda t: xs(X, b, t * P, P), b_mv, b_rs[:, TB:2 * TB]).then_inc(z_ready, 1)
                if j == 7:
                    dve.wait_ge(score_ready, k)
                    link(dve.tensor_reduce(m1[:, :], sc, AX.X, ALU.max))
                    link(dve.tensor_tensor(v(e1), sc, over(m1[:, :], E), ALU.is_equal))
                    link(dve.tensor_tensor(e1[:, :], e1[:, :], prio[:, :], ALU.mult))
                    link(dve.tensor_reduce(pm[:, :], v(e1), AX.X, ALU.max))
                if j == 8:
                    link(dve.tensor_tensor(v(oh1), v(e1), over(pm[:, :], E), ALU.is_equal))
                    link(dve.scalar_tensor_tensor(v(rest), v(oh1), -HUGE, sc, ALU.mult, ALU.add))
                    link(dve.tensor_reduce(m2[:, :], v(rest), AX.X, ALU.max))
                if j == 9:
                    if l == 0:
                        dve.tensor_tensor(w1[:, :], m1[:, :], m2[:, :], ALU.subtract).then_inc(d_ready, 1)
                    link(dve.tensor_tensor(v(e1), v(rest), over(m2[:, :], E), ALU.is_equal))
                    link(dve.tensor_tensor(e1[:, :], e1[:, :], prio[:, :], ALU.mult))
                    link(dve.tensor_reduce(pm[:, :], v(e1), AX.X, ALU.max))
                    if l == 1:
                        dve.tensor_tensor(v(rest), sc, over(m1[:, :], E), ALU.subtract).then_inc(d_ready, 1)
                if j == 10:
                    link(dve.tensor_tensor(v(oh2), v(e1), over(pm[:, :], E), ALU.is_equal))
                    if l == 1:
                        link(dve.tensor_tensor(oh1[:, :], oh1[:, :], oh2[:, :], ALU.add))
                if j == 6:
                    dve.wait_ge(xh_ready, k)
                    dve.tensor_tensor(xs(xL, b), zT[:, :], xs(xH, b).bitcast(F32), ALU.subtract).then_inc(xl_ready, 1)
                if j == 11:
                    dve.wait_ge(th_ready, k)
                    if l == 0:
                        link(dve.tensor_scalar(w1[:, :], th[:, 0:TB], 0.25, 0.25, ALU.mult, ALU.add))
                        link(dve.tensor_scalar(w2[:, :], th[:, 0:TB], -0.25, 0.25, ALU.mult, ALU.add))
                    else:
                        link(dve.tensor_scalar(thn[:, :], th[:, :], -1.0, 1.0, ALU.mult, ALU.add))
                        link(dve.reciprocal(thn[:, :], thn[:, :]))
                        link(dve.scalar_tensor_tensor(rest[:, :], th[:, :], 1.0, thn[:, :], ALU.add, ALU.mult))
                if j == 12:
                    if l == 0:
                        link(dve.tensor_tensor(v(oh1), v(oh1), over(w1[:, :], E), ALU.mult))
                        link(dve.tensor_tensor(v(oh2), v(oh2), over(w2[:, :], E), ALU.mult))
                        dve.tensor_tensor(wt[:, :], oh1[:, :], oh2[:, :], ALU.add).then_inc(w_ready, 1)
                    else:
                        link(dve.tensor_reduce(w1[:, :], v(rest), AX.X, ALU.add))
                        link(dve.reciprocal(w2[:, :], w1[:, :]))
                        link(dve.scalar_tensor_tensor(rest[:, :], rest[:, :], 0.5, oh1[:, :], ALU.mult, ALU.mult))
                        dve.tensor_tensor(v(wt), v(rest), over(w2[:, :], E), ALU.mult).then_inc(w_ready, 1)
                if j == SKIP_AT:
                    link(dve.tensor_scalar(b_mul[:, :], b_rs[:, 0:TB], 0.5, 1.0, ALU.mult, ALU.add))
                    dve.scalar_tensor_tensor(b_add[:, :], b_mv[:, 0:2 * TB:2], -0.5, b_rs[:, 0:TB], ALU.mult, ALU.mult).then_inc(skip_ready, 1)
                if j == SKIP_AT + 2:
                    dve.wait_ge(skip_ready, k)
                    for t in range(TB):
                        last = dve.tensor_scalar(xs(X, b, t * P, P), xs(X, b, t * P, P), b_mul[:, t:t + 1], b_add[:, t:t + 1],
                                                 ALU.mult, ALU.add)
                    link(last, apart=spare[:, 0:1])
                    assert link.n == LINKS_B[l], (l, link.n)

            def after_stage(s, b, j, link):
                if j == LAG:
                    m = NB * s + b
                    dve.wait_ge(acc_tok, m + 1)
                    ins = dve.tensor_tensor(xs(X, b), xs(X, b), S[0][:, :], ALU.add)
                    if s in (0, 2):
                        link(ins, apart=spare[:, 0:1])
                    else:
                        ins.then_inc(x_done, 1)

            def att_after(l, s, b, j, ka, link):
                if j in (LAG, LAG + 1):
                    stats(link, lambda t: xs(X, b, t * P, P), a_st, a_mv, a_ve, 1e-5 if l == 0 else None, False, ln1_var,
                          part=(j - LAG,))
                if j == 6:
                    dve.wait_ge(ln1_rstd, ka + 4 * l)
                    normalise(R[0], lambda t: xs(X, b, t * P, P), a_mv, a_rs).then_inc(yn_ready, 1)
                if l == 0:
                    if j == 9:
                        dve.wait_ge(proj_used, 5 * ka - 4)
                        link(dve.tensor_scalar(R[1], R[0], cols0[:, 5:6], cols0[:, 7:8], ALU.mult, ALU.add))
                        dve.tensor_scalar(R[0], R[0], cols0[:, 6:7], cols0[:, 8:9], ALU.mult, ALU.add).then_inc(qk_ready, 1)
                    if j in (11, 12):
                        q = j - 11
                        dve.wait_ge(relu_ready, 2 * ka - 1 + q)
                        dve.tensor_tensor(R[6 + q], R[6 + q], R[6 + q], ALU.mult).then_inc(sq_ready, 1)
                    if j in (13, 14):
                        q = j - 13
                        dve.wait_ge(av_ready, 2 * ka - 1 + q)
                        g = tiles(region[:, 2 * NT:4 * NT], NT)[:, :, q * SEQ:(q + 1) * SEQ]
                        dve.tensor_tensor(g, tiles(S[1 - q][:, :], SEQ), g, ALU.mult).then_inc(og_ready, 1)
                    if j == 15:
                        dve.wait_ge(ao_ready, ka)
                        dve.tensor_tensor(xs(X, b), xs(X, b), S[1][:, :], ALU.add).then_inc(x_done, 1)
                        assert link.n == LINKS_A[0], link.n
                else:
                    if j in (9, 10):
                        q = j - 9
                        dve.wait_ge(qkv_ready, 2 * ka - 1 + q)
                        dve.tensor_scalar(tiles(R[2][:, q * SEQ:(q + 1) * SEQ]), tiles(S[q][:, :], 2 * P)[:, :, 0:P], 0.0, None,
                                          ALU.min).then_inc(min_ready, 1)
                    if j == 12:
                        dve.wait_ge(exp_ready, ka)
                        for q in range(2):
                            last = dve.scalar_tensor_tensor(tiles(R[0][:, q * SEQ:(q + 1) * SEQ]), tiles(S[q][:, :], 2 * P)[:, :, 0:P],
                                                            0.0, tiles(R[2][:, q * SEQ:(q + 1) * SEQ]), ALU.max, ALU.add)
                        last.then_inc(phi_ready, 1)
                    if j == 15:
                        dve.wait_ge(kcum_ready, ka)
                        dve.tensor_tensor(tiles(kden[:, :], 64), tiles(S[0][:, 0:TB * 64], 64), tiles(R[0])[:, :, 0:64], ALU.mult).then_inc(den_read, 1)
                        dve.wait_ge(den_read, ka)
                        link(dve.tensor_reduce(den[:, :], kden[:, :].rearrange("p (a f) -> p a f", f=F), AX.X, ALU.add))
                        link(dve.tensor_scalar(den[:, :], den[:, :], 1e-6, None, ALU.add))
                        link(dve.reciprocal(rden[:, :], den[:, :]))
                    if j in (16, 17, 18, 19):
                        t = j - 16
                        dve.wait_ge(cum_ready, 4 * ka - 3 + t)
                        qq = R[0][:, t * P:t * P + 64].rearrange("p (h f) -> p h f", f=F)
                        dve.tensor_tensor(R[2].rearrange("p (h f g) -> p h f g", f=F, g=G),
                                          S[(t + 1) % 2][:, :].rearrange("p (h f g) -> p h f g", f=F, g=G),
                                          qq.unsqueeze(3).to_broadcast([P, HEADS, F, G]), ALU.mult).then_inc(cum_used, 1)
                        dve.wait_ge(cum_used, 4 * ka - 3 + t)
                        link(dve.tensor_reduce(xT[:, t * P:(t + 1) * P].rearrange("p (h g) -> p h g", g=G),
                                               R[2].rearrange("p (h f g) -> p h g f", f=F, g=G), AX.X, ALU.add))
                    if j == 19:
                        o = xT[:, :].rearrange("p (a g) -> p a g", g=G)
                        dve.tensor_tensor(o, o, over(rden[:, :], G), ALU.mult).then_inc(att_ready, 1)
                    if j == 21:
                        dve.wait_ge(ao_ready, NB + ka)
                        assert link.n == LINKS_A[1], link.n
                        dve.tensor_tensor(xs(X, b), xs(X, b), S[0][:, :], ALU.add).then_inc(x_done, 1)

            def sides(s, b, j, state):
                sa, ba = side_after(s, b)
                if sa >= 0:
                    if sa in (0, 2) and j == 0:
                        base = ba * LINKS_A[0] if sa == 0 else NB * LINKS_A[0] + ba * LINKS_A[1]
                        state["alink"] = Links(dve, a_link, base)
                    after_stage(sa, ba, j, state.get("alink"))
                a_first = j in (6, 9, 10)
                if sa in (0, 2) and a_first:
                    att_after(sa // 2, sa, ba, j, ba + 1, state["alink"])
                sb_, bb = side_before(s, b)
                if 0 <= sb_ < 3:
                    k = NB * (sb_ + 1) + bb + 1
                    if j == 0:
                        after_apart(dve, spare[:, 0:1], x_done, k - NB)
                    before(layer[sb_ + 1], j, k, bb, state)
                if sa in (0, 2) and not a_first:
                    att_after(sa // 2, sa, ba, j, ba + 1, state["alink"])
                for blk, js in first_prep(s, b, j):
                    if js[0] == 0 and blk == 1:
                        dve.wait_ge(x1_loaded, 16)
                    if js[0] == 0 and blk == 2:
                        dve.wait_ge(x_rest_loaded, 16 * (NB - 2))
                    for j_ in js:
                        before(0, j_, blk + 1, blk, state)
                if s == 0 and isinstance(b, int) and b == 0 and j == BIAS_AT + 1:
                    dve.wait_ge(bias_hi, 1)
                    dve.scalar_tensor_tensor(brows[:, :], brows[:, :].bitcast(F32), row1[:, 0:1], region[0:2, 5 * NT:5 * NT + BIAS],
                                             ALU.mult, ALU.add).then_inc(bias_split, 1)

            dve.wait_ge(x_loaded, 16)
            dve.wait_ge(consts, 6)
            first_state = {}
            for j in range(TAIL):
                before(0, j, 1, 0, first_state)
            done = [len(pieces0)]

            def to_lo(n, l, lp, j):
                dve.wait_ge(hi_done, n + 1)
                dve.tensor_tensor(in_ring(hL, l, j), hid_ring(l, j), in_ring(hH, l, j).bitcast(F32),
                                  ALU.subtract).then_inc(lo_done, 1)

            def body(s, b):
                ex = experts[layer[s]]
                n = step_of(s, b)
                state = first_state if s == 0 and isinstance(b, int) and b == 0 else {}
                for j in range(steps[s]):
                    early = side_after(s, b)[0] == 2 and 16 <= j <= 19
                    if early:
                        sides(s, b, j, state)
                    dve.wait_ge(silu_done, n + j + 1)
                    h = hid_ring(layer[s], j)
                    dve.tensor_tensor(h, UG[j % 2][:, 0:NT], h, ALU.mult).then_inc(hid_done, 1)
                    if not early:
                        sides(s, b, j, state)
                    to_split(to_lo, s, b, j)
                    if splits_at(s, b, j):
                        split_lo_piece(done[0])
                        done[0] += 1

            each_body(dve, body)
            for j in range(SPLIT_LAG):
                to_split(to_lo, 4, 0, j)
            sides(4, 0, LAG, {})

        @block.tensor
        def _(pe):
            def before(l, j, k):
                if j == 4:
                    pe.wait_ge(z_ready, k)
                    after(pe, wT_used, k - 1)
                    for t in range(TB):
                        last = pe.transpose(S[2][:, t * P:(t + 1) * P], Z[:, t * P:(t + 1) * P], ident[:, :])
                    last.then_inc(zT_ready, 1)
                if j == 6:
                    pe.wait_ge(xh_ready, k)
                    for t in range(TB):
                        last = pe.matmul(S[2][:, t * E:(t + 1) * E], zT[:, t * P:(t + 1) * P], wr[:, l * E:(l + 1) * E],
                                         start=True, stop=True)
                    last.then_inc(score_ready, 1)
                if j == 14:
                    pe.wait_ge(w_ready, k)
                    pe.transpose(S[2][0:TB * E, 0:P], wt[:, :], ident[:, :]).then_inc(wT_ready, 1)

            def after_stage(s, b, j):
                if j == LAG:
                    m = NB * s + b
                    pe.wait_ge(accT, m + 1)
                    after(pe, x_done, m)
                    for t in range(TB):
                        last = pe.transpose(S[0][:, t * P:(t + 1) * P], R[3][:, t * P:(t + 1) * P], ident[:, :])
                    last.then_inc(acc_tok, 1)

            def att_after(l, j, ka):
                if j == 7:
                    pe.wait_ge(yn_ready, ka + 4 * l)
                    for t in range(TB):
                        last = pe.transpose(S[1][:, t * P:(t + 1) * P], R[0][:, t * P:(t + 1) * P], ident[:, :])
                    last.then_inc(ynT_ready, 1)
                if l == 0:
                    if j == 8:
                        pe.wait_ge(xT_ready, ka)
                        pe.matmul(S[0][:, :], w_qk[:, :], xT[:, :], start=True, stop=True).then_inc(proj_ready, 1)
                    if j in (8, 9):
                        c = j - 8
                        if c:
                            pe.wait_ge(proj_used, 5 * ka - 4)
                        pe.matmul(S[1 - c][:, :], w_hid[:, HID + c * P:HID + (c + 1) * P], xT[:, :], start=True, stop=True).then_inc(proj_ready, 1)
                    if j in (9, 10):
                        q = j - 9
                        pe.wait_ge(proj_used, 5 * ka - 3 + q)
                        for t in range(2):
                            o = S[1 - q][:, t * HID:(t + 1) * HID]
                            pe.matmul(o, xT[:, (2 * q + t) * P:(2 * q + t + 1) * P], w_hid[:, 0:HID], start=True, stop=False)
                            last = pe.matmul(o, onesR[:, :], bias_v, start=False, stop=True)
                        last.then_inc(proj_ready, 1)
                    if j in (10, 11):
                        q = j - 10
                        pe.wait_ge(proj_used, 5 * ka - 1 + q)
                        pe.wait_ge(qk_ready, ka)
                        for t in range(2):
                            last = pe.matmul(S[1 - q][:, t * SEQ:(t + 1) * SEQ], R[0][:, q * SEQ + t * P:q * SEQ + (t + 1) * P],
                                             R[1][:, q * SEQ:(q + 1) * SEQ], start=True, stop=True)
                        last.then_inc(sim_ready, 1)
                    if j in (12, 13):
                        q = j - 12
                        pe.wait_ge(sq_ready, 2 * ka - 1 + q)
                        for c in range(2):
                            for t in range(2):
                                last = pe.matmul(S[1 - q][:, c * SEQ:(c + 1) * SEQ], R[4 + q][:, t * HID + c * P:t * HID + (c + 1) * P],
                                                 R[6 + q][:, t * SEQ:(t + 1) * SEQ], start=(t == 0), stop=(t == 1))
                        last.then_inc(av_ready, 1)
                    if j == 15:
                        pe.wait_ge(og_ready, 2 * ka)
                        for t in range(TB):
                            o = S[1][:, t * P:(t + 1) * P]
                            for c in range(2):
                                pe.matmul(o, R[2 + c][:, t * P:(t + 1) * P], w_o0[:, c * P:(c + 1) * P], start=(c == 0), stop=False)
                            last = pe.matmul(o, onesR[:, :], bias_o0, start=False, stop=True)
                        last.then_inc(ao_ready, 1)
                else:
                    if j in (8, 9):
                        q = j - 8
                        pe.wait_ge(xT_ready, NB + ka)
                        for t in range(2):
                            o = S[q][:, t * 2 * P:(t + 1) * 2 * P]
                            pe.matmul(o, xT[:, (2 * q + t) * P:(2 * q + t + 1) * P], w_qkv[:, :], start=True, stop=False)
                            last = pe.matmul(o, onesR[:, :], bias_qkv, start=False, stop=True)
                        last.then_inc(qkv_ready, 1)
                    if j == 14:
                        pe.wait_ge(phi_ready, ka)
                        for t in range(TB):
                            o = S[0][:, t * 64:(t + 1) * 64]
                            last = pe.matmul(o, tri[:, :], R[0][:, t * P + 64:(t + 1) * P], start=True, stop=(t % 2 == 0))
                            if t % 2:
                                last = pe.matmul(o, ones[:, :], R[0][:, (t - 1) * P + 64:t * P], start=False, stop=True)
                        last.then_inc(kcum_ready, 1)
                    if j in (15, 16, 17, 18):
                        t = j - 15
                        pe.wait_ge(kv_ready, 4 * ka - 3 + t)
                        if t == 0:
                            pe.wait_ge(v_ready, 2 * ka)
                        if t == 1:
                            pe.wait_ge(den_read, ka)
                        if t >= 2:
                            pe.wait_ge(cum_used, 4 * ka - 5 + t)
                        o = S[(t + 1) % 2][:, :]
                        last = pe.matmul(o, tri[:, :], R[3 + t], start=True, stop=(t % 2 == 0))
                        if t % 2:
                            last = pe.matmul(o, ones[:, :], R[2 + t], start=False, stop=True)
                        last.then_inc(cum_ready, 1)
                    if j == 20:
                        pe.wait_ge(att_ready, ka)
                        for t in range(TB):
                            last = pe.transpose(S[1][:, t * P:(t + 1) * P], xT[:, t * P:(t + 1) * P], ident[:, :])
                        last.then_inc(attT_ready, 1)
                    if j == 21:
                        pe.wait_ge(attT_used, ka)
                        for t in range(TB):
                            o = S[0][:, t * P:(t + 1) * P]
                            pe.matmul(o, R[1][:, t * P:(t + 1) * P], w_o1[:, :], start=True, stop=False)
                            last = pe.matmul(o, onesR[:, :], bias_o1, start=False, stop=True)
                        last.then_inc(ao_ready, 1)

            def sides(s, b, j):
                sa, ba = side_after(s, b)
                if sa >= 0:
                    after_stage(sa, ba, j)
                if sa in (0, 2):
                    att_after(sa // 2, j, ba + 1)
                sb_, bb = side_before(s, b)
                if 0 <= sb_ < 3:
                    before(layer[sb_ + 1], j, NB * (sb_ + 1) + bb + 1)
                for blk, js in first_prep(s, b, j):
                    for j_ in js:
                        before(0, j_, blk + 1)

            pe.wait_ge(consts, 6)
            pe.wait_ge(norm_loaded, 32)
            for j in range(TAIL):
                before(0, j, 1)

            def down(l, n, j):
                ex = experts[l]
                pe.wait_ge(lo_done, n + 1)
                if j == 0:
                    after(pe, accT, block_of[0])
                wh, wl = downH[l][:, j * P:(j + 1) * P], downL[l][:, j * P:(j + 1) * P]
                hh, hl = in_ring(hH, l, j), in_ring(hL, l, j)
                pe.matmul(ACC[:, :], wh, hh, start=(j == 0), stop=False)
                pe.matmul(ACC[:, :], wh, hl, start=False, stop=False)
                pe.matmul(ACC[:, :], wl, hh, start=False, stop=(j == ex.steps - 1)).then_inc(down_done, 1)

            block_of = [0]

            def body(s, b):
                l = layer[s]
                ex = experts[l]
                n = step_of(s, b)
                block_of[0] = NB * s + b
                for j in range(steps[s]):
                    if j == 0:
                        pe.wait_ge(xl_ready, NB * s + b + 1)
                    if s == 0 and isinstance(b, int) and b == 0 and j % 2 == 0:
                        pe.wait_ge(split_lo0, up_piece[j // 2] + 1)
                    if s == 2 and isinstance(b, int) and b == 0 and j == 0:
                        pe.wait_ge(split_lo1, len(pieces1))
                    after(pe, hid_done, n + j - 1)
                    for half in range(2):
                        cols = slice((2 * j + half) * P, (2 * j + half + 1) * P)
                        o = UG[j % 2][:, half * NT:(half + 1) * NT]
                        pe.matmul(o, upH[l][:, cols], xs(xH, b), start=True, stop=False)
                        pe.matmul(o, upH[l][:, cols], xs(xL, b), start=False, stop=False)
                        last = pe.matmul(o, upL[l][:, cols], xs(xH, b), start=False, stop=True)
                    last.then_inc(up_done, 1)
                    if j >= LAG:
                        if s == 0 and isinstance(b, int) and b == 0:
                            if (j - LAG) % 4 == 0:
                                pe.wait_ge(split_lo0, down_piece[(j - LAG) // 4] + 1)
                            if j == steps[0] - 1:
                                pe.wait_ge(split_lo0, len(pieces0))
                                pe.wait_ge(bias_split, 1)
                        down(l, n + j - LAG, j - LAG)
                    elif prev_layer(s, b) is not None:
                        down(prev_layer(s, b), n + j - LAG, steps[side_after(s, b)[0]] + j - LAG)
                    sides(s, b, j)

            each_body(pe, body)
            for j in range(LAG):
                down(1, first_step[4] + j - LAG, steps[3] + j - LAG)
            sides(4, 0, LAG)


_OUTS = [((8, 256, 128), "float32")]


def kernel(**inputs):
    import numpy as np
    import concourse.bacc as bacc
    from concourse.bass_utils import run_bass_kernel_spmd

    g = {k: np.asarray(v) for k, v in inputs.items()}

    def up(w):
        e, h2, d = w.shape
        return w.reshape(e, 2, h2 // 2, d).transpose(3, 0, 2, 1).reshape(d, -1, P, 2).transpose(0, 1, 3, 2).reshape(d, -1)

    def down(w):
        e, d, h = w.shape
        return w.transpose(0, 2, 1).reshape(e * h // P, P, d).transpose(1, 0, 2).reshape(P, -1)

    def cols(*vectors):
        return np.stack(vectors, axis=1)

    bh, osw, osb = g["L0_attn_b_hidden"], g["L0_attn_os_weight"], g["L0_attn_os_bias"]
    arrays = {
        "x": g["L0_attn_x"].reshape(-1, P),
        "up0": up(g["L0_ffn_w_up"]),
        "down0": down(g["L0_ffn_w_down"]),
        "up1": up(g["L1_ffn_w_up"]),
        "down1": down(g["L1_ffn_w_down"]),
        "router": np.concatenate([g["L0_ffn_w_router"].T, g["L1_ffn_w_router"].T], axis=1),
        "norm": cols(g["L0_ffn_norm_scale"], g["L1_ffn_norm_scale"]),
        "att0_w": g["L0_attn_W_hidden"],
        "att0_qk": g["L0_attn_W_qk"],
        "att0_out": g["L0_attn_W_out"].reshape(2, P, P).transpose(1, 0, 2).reshape(P, 2 * P),
        "att0_cols": cols(g["L0_attn_ln_scale"], g["L0_attn_ln_bias"], g["L0_attn_b_qk"], bh[HID:HID + P], bh[HID + P:],
                          osw[0], osw[1], osb[0], osb[1]),
        "att1_w": np.concatenate([g["L1_attn_wq"], g["L1_attn_wk"], g["L1_attn_wv"]], axis=1),
        "att1_out": g["L1_attn_wo"],
        "bias_rows": np.stack([np.concatenate([bh[:HID], g["L0_attn_b_out"], g["L1_attn_bq"], g["L1_attn_bk"],
                                               g["L1_attn_bv"], g["L1_attn_bo"]])] * 2),
    }
    nc = bacc.Bacc("TRN2", target_bir_lowering=False, num_devices=1)
    feed, args = {}, []
    for name, a in arrays.items():
        a = np.ascontiguousarray(a)
        feed[f"in_{name}"] = a
        args.append(nc.dram_tensor(f"in_{name}", a.shape, mybir.dt.from_np(a.dtype), kind="ExternalInput").ap())
    args.append(nc.dram_tensor("out", [2048, P], F32, kind="ExternalOutput").ap())
    macaron(nc, *args)
    r = run_bass_kernel_spmd(nc, [feed], core_ids=[0])
    return r.results[0]["out"].reshape(8, 256, 128)
```
